# Optimizing a Trainium2 kernel written in Bass

```python
import numpy as np
import jax
import jax.numpy as jnp

def _softmax(x, axis=-1):
    return jax.nn.softmax(x, axis=axis)

def _gelu(x):
    return jax.nn.gelu(x, approximate=True)

def _silu(x):
    return jax.nn.silu(x)

def _sigmoid(x):
    return jax.nn.sigmoid(x)

def _layernorm(x, axis=-1, eps=1e-05):
    m = jnp.mean(x, axis=axis, keepdims=True)
    v = jnp.var(x, axis=axis, keepdims=True)
    return (x - m) / jnp.sqrt(v + eps)

def _scatter_add(tgt, idx, src, axis=0):
    return tgt.at[idx].add(src)

def _segment_sum(src, seg, n):
    return jax.ops.segment_sum(src, seg, n)
kernel_name = 'mk_xattn_ffn_d1_seqx_r4_bcf1e5'

def setup_inputs(seed: int=0):
    np.random.seed(seed)
    _w = jnp.asarray

    def _rec_inputs():
        import jax
        import jax.numpy as jnp
        _rk = jax.random.key(seed)
        x = 0.000341 + 1 * jax.random.normal(jax.random.fold_in(_rk, 1), (16, 256, 512), jnp.float32)
        _lenS = 256 - jax.random.randint(jax.random.fold_in(_rk, 7), (16,), 0, max(1, 256 // 4) + 1, jnp.int32)
        _lenS2 = 256 - jax.random.randint(jax.random.fold_in(_rk, 8), (16,), 0, max(1, 256 // 4) + 1, jnp.int32)
        _ctx_2048P = jax.random.normal(jax.random.fold_in(_rk, 11), (16, 16, 512), jnp.float32)
        _ctx_2048c = jax.random.dirichlet(jax.random.fold_in(_rk, 511), 0.3 * jnp.ones((16,), jnp.float32), (16, 256))
        _ctx_2048t = jnp.einsum('bsk,bkd->bsd', _ctx_2048c, _ctx_2048P)
        _ctx_2048t = _ctx_2048t * jax.lax.rsqrt(jnp.mean(jnp.square(_ctx_2048t)) + 1e-12) * 0.953939
        ctx_2048 = -1.47943e-05 + 1.00017 * (_ctx_2048t + 0.3 * jax.random.normal(jax.random.fold_in(_rk, 611), (16, 256, 512), jnp.float32))
        return (x, ctx_2048)
    x, ctx_2048 = _rec_inputs()

    def _L0_xattn_setup():
        import jax, jax.numpy as jnp
        import numpy as np

        def _wkv(time_decay, time_first, k, v):
            w = -jnp.exp(time_decay)
            u = time_first
            B, T, C = k.shape
            aa = jnp.zeros((B, C), dtype=k.dtype)
            bb = jnp.zeros((B, C), dtype=k.dtype)
            pp = jnp.full((B, C), -1e+38, dtype=k.dtype)

            def step(carry, kv_t):
                aa, bb, pp = carry
                kt, vt = kv_t
                ww = u + kt
                q = jnp.maximum(pp, ww)
                e1 = jnp.exp(pp - q)
                e2 = jnp.exp(ww - q)
                y_t = (e1 * aa + e2 * vt) / (e1 * bb + e2)
                ww2 = pp + w
                q2 = jnp.maximum(ww2, kt)
                e1b = jnp.exp(ww2 - q2)
                e2b = jnp.exp(kt - q2)
                new_carry = (e1b * aa + e2b * vt, e1b * bb + e2b, q2)
                return (new_carry, y_t)
            ks = jnp.transpose(k, (1, 0, 2))
            vs = jnp.transpose(v, (1, 0, 2))
            _, ys = jax.lax.scan(step, (aa, bb, pp), (ks, vs))
            return jnp.transpose(ys, (1, 0, 2))
        key = jax.random.key(seed)
        k1, k2, k3, k4 = jax.random.split(key, 4)
        B, T, C = (8, 256, 512)
        return {'batch_size': B, 'seq_len': T, 'embedding_dim': C, 'time_decay': jax.random.normal(k1, (C,), dtype=jnp.float32), 'time_first': jax.random.normal(k2, (C,), dtype=jnp.float32), 'k': jax.random.normal(k3, (B, T, C), dtype=jnp.float32), 'v': jax.random.normal(k4, (B, T, C), dtype=jnp.float32)}
    _L0_xattn_all = _L0_xattn_setup()
    _L0_xattn_in = {k: v for k, v in _L0_xattn_all.items() if k in ('time_decay', 'time_first')}
    del _L0_xattn_all

    def _L0_ffn_setup():
        import jax, jax.numpy as jnp
        import numpy as np
        BLOCK = 64

        def dequant4bit(q, scale):
            return (q.astype(jnp.float32) - 7.5) * jnp.repeat(scale, BLOCK, axis=1)
        key = jax.random.key(seed)
        ks = jax.random.split(key, 11)
        B, S, D, H, R = (4, 512, 512, 2048, 16)
        return {'x1': jax.random.normal(ks[0], (B, S, D), jnp.float32), 'w_up_q': jax.random.randint(ks[1], (H, D), 0, 16, dtype=jnp.int32), 'w_up_scale': jax.random.uniform(ks[2], (H, D // BLOCK), jnp.float32) * 0.02, 'b_up': jax.random.normal(ks[3], (H,), jnp.float32) * 0.01, 'w_up_lora_a': jax.random.normal(ks[4], (D, R), jnp.float32) * 0.02, 'w_up_lora_b': jax.random.normal(ks[5], (R, H), jnp.float32) * 0.02, 'w_down_q': jax.random.randint(ks[6], (D, H), 0, 16, dtype=jnp.int32), 'w_down_scale': jax.random.uniform(ks[7], (D, H // BLOCK), jnp.float32) * 0.02, 'b_down': jax.random.normal(ks[8], (D,), jnp.float32) * 0.01, 'w_down_lora_a': jax.random.normal(ks[9], (H, R), jnp.float32) * 0.02, 'w_down_lora_b': jax.random.normal(ks[10], (R, D), jnp.float32) * 0.02}
    _L0_ffn_all = _L0_ffn_setup()
    _L0_ffn_in = {k: v for k, v in _L0_ffn_all.items() if k in ('w_up_q', 'w_up_scale', 'b_up', 'w_up_lora_a', 'w_up_lora_b', 'w_down_q', 'w_down_scale', 'b_down', 'w_down_lora_a', 'w_down_lora_b')}
    del _L0_ffn_all
    return {'x': x, 'ctx_2048': ctx_2048, 'L0_xattn_time_decay': _L0_xattn_in['time_decay'], 'L0_xattn_time_first': _L0_xattn_in['time_first'], 'L0_ffn_w_up_q': _L0_ffn_in['w_up_q'], 'L0_ffn_w_up_scale': _L0_ffn_in['w_up_scale'], 'L0_ffn_b_up': _L0_ffn_in['b_up'], 'L0_ffn_w_up_lora_a': _L0_ffn_in['w_up_lora_a'], 'L0_ffn_w_up_lora_b': _L0_ffn_in['w_up_lora_b'], 'L0_ffn_w_down_q': _L0_ffn_in['w_down_q'], 'L0_ffn_w_down_scale': _L0_ffn_in['w_down_scale'], 'L0_ffn_b_down': _L0_ffn_in['b_down'], 'L0_ffn_w_down_lora_a': _L0_ffn_in['w_down_lora_a'], 'L0_ffn_w_down_lora_b': _L0_ffn_in['w_down_lora_b']}

def reference(x, ctx_2048, L0_xattn_time_decay, L0_xattn_time_first, L0_ffn_w_up_q, L0_ffn_w_up_scale, L0_ffn_b_up, L0_ffn_w_up_lora_a, L0_ffn_w_up_lora_b, L0_ffn_w_down_q, L0_ffn_w_down_scale, L0_ffn_b_down, L0_ffn_w_down_lora_a, L0_ffn_w_down_lora_b):
    import jax
    import jax.numpy as jnp

    def _L0_xattn_ref(batch_size, seq_len, embedding_dim, time_decay, time_first, k, v):
        import jax, jax.numpy as jnp
        import numpy as np

        def _wkv(time_decay, time_first, k, v):
            w = -jnp.exp(time_decay)
            u = time_first
            B, T, C = k.shape
            aa = jnp.zeros((B, C), dtype=k.dtype)
            bb = jnp.zeros((B, C), dtype=k.dtype)
            pp = jnp.full((B, C), -1e+38, dtype=k.dtype)

            def step(carry, kv_t):
                aa, bb, pp = carry
                kt, vt = kv_t
                ww = u + kt
                q = jnp.maximum(pp, ww)
                e1 = jnp.exp(pp - q)
                e2 = jnp.exp(ww - q)
                y_t = (e1 * aa + e2 * vt) / (e1 * bb + e2)
                ww2 = pp + w
                q2 = jnp.maximum(ww2, kt)
                e1b = jnp.exp(ww2 - q2)
                e2b = jnp.exp(kt - q2)
                new_carry = (e1b * aa + e2b * vt, e1b * bb + e2b, q2)
                return (new_carry, y_t)
            ks = jnp.transpose(k, (1, 0, 2))
            vs = jnp.transpose(v, (1, 0, 2))
            _, ys = jax.lax.scan(step, (aa, bb, pp), (ks, vs))
            return jnp.transpose(ys, (1, 0, 2))
        assert seq_len <= 256
        return _wkv(time_decay, time_first, k, v)

    def _L0_ffn_ref(x1, w_up_q, w_up_scale, b_up, w_up_lora_a, w_up_lora_b, w_down_q, w_down_scale, b_down, w_down_lora_a, w_down_lora_b):
        import jax, jax.numpy as jnp
        import numpy as np
        BLOCK = 64

        def dequant4bit(q, scale):
            return (q.astype(jnp.float32) - 7.5) * jnp.repeat(scale, BLOCK, axis=1)
        w_up = dequant4bit(w_up_q, w_up_scale).T
        y1 = x1 @ w_up + b_up + x1 @ w_up_lora_a @ w_up_lora_b
        x2 = jax.nn.relu(y1)
        w_down = dequant4bit(w_down_q, w_down_scale).T
        y2 = x2 @ w_down + b_down + x2 @ w_down_lora_a @ w_down_lora_b
        return y2
    x = x + _L0_xattn_ref(16, 256, 512, L0_xattn_time_decay, L0_xattn_time_first, _layernorm(x, axis=-1), ctx_2048)
    x = x + _L0_ffn_ref(_layernorm(x, axis=-1), L0_ffn_w_up_q, L0_ffn_w_up_scale, L0_ffn_b_up, L0_ffn_w_up_lora_a, L0_ffn_w_up_lora_b, L0_ffn_w_down_q, L0_ffn_w_down_scale, L0_ffn_b_down, L0_ffn_w_down_lora_a, L0_ffn_w_down_lora_b)
    return x

_drawn_inputs = setup_inputs


def setup_inputs(seed=0):
    import zlib

    import numpy as np

    out = dict(_drawn_inputs(seed))
    spreads = {}
    factors = {'L0_ffn_b_up': 8.0, 'L0_ffn_b_down': 8.0}
    for name, (base, spread) in spreads.items():
        noise = np.random.default_rng([zlib.crc32(name.encode()), seed]).standard_normal(out[name].shape)
        drawn = base * np.exp(spread * noise) if base else spread * noise
        out[name] = jnp.asarray(drawn.astype(out[name].dtype))
    for name, factor in factors.items():
        out[name] = (out[name] * factor).astype(out[name].dtype)
    return out
```

```python
from contextlib import ExitStack

import concourse.bass as bass
from concourse import mybir

F32 = mybir.dt.float32
F32R = mybir.dt.float32r
I32 = mybir.dt.int32
ALU = mybir.AluOpType
ACT = mybir.ActivationFunctionType

P = 128
BATCH = 16
SEQ = 256
D = 512
HID = 2048
RANK = 16
BLOCK = 64
ZERO = 7.5
EPS = 1e-5
PAIR = 2 * SEQ
NPAIR = BATCH * SEQ // PAIR
KT = D // P
HT = HID // P
JT = PAIR // P
NB = D // BLOCK
DB = KT * (P // BLOCK)
LORA_DN = 32
BN = 6


def build(nc, x, ctx_t, decay, first, q_up, s_up, b_up, lora_rows, lora_cols, q_dn, s_dn, b_dn, out):
    xt = x.rearrange("(n j p) d -> n j p d", p=P, j=JT)
    ot = out.rearrange("(n j p) d -> n j p d", p=P, j=JT)
    vt = ctx_t.rearrange("(c p) (n t) -> n c p t", p=P, t=PAIR)

    with ExitStack() as ctx:
        def sb(name, shape, dt=F32):
            return ctx.enter_context(nc.sbuf_tensor(name, shape, dt))

        def psum(name):
            return ctx.enter_context(nc.psum_tensor(name, [P, 512], F32))

        def sem(name):
            return ctx.enter_context(nc.semaphore(name))

        up_hi = sb("up_hi", [P, KT, HID], F32R)
        up_lo = sb("up_lo", [P, KT, HID], F32R)
        dn_hi = sb("dn_hi", [P, HT, D], F32R)
        dn_lo = sb("dn_lo", [P, HT, D], F32R)
        wq_up = sb("wq_up", [P, 2, D])
        wq_dn = sb("wq_dn", [P, 2, D])
        sc_up = sb("sc_up", [P, HT, NB])
        sc_dn = sb("sc_dn", [P, HT, DB])
        lo_rows = sb("lo_rows", [LORA_DN + RANK, D])
        lo_cols = sb("lo_cols", [LORA_DN + RANK, 2, P])
        bias_up = sb("bias_up", [P, HT])
        bias_dn = sb("bias_dn", [P, D])
        ident = sb("ident", [P, P])
        par = sb("par", [P, 2, KT])
        base = sb("base", [P, KT])
        half = sb("half", [P, JT])
        eps = sb("eps", [P, JT])
        expo = sb("expo", [P, 3, KT])
        omega = sb("omega", [P, KT])
        alpha = sb("alpha", [P, KT])
        beta = sb("beta", [P, KT])
        xin = sb("xin", [P, JT, D])
        mix = sb("mix", [P, JT, D])
        res = sb("res", [P, JT, D])
        st1 = sb("st1", [P, JT, BN])
        st2 = sb("st2", [P, JT, BN])
        mv1 = sb("mv1", [P, JT, 2])
        mv2 = sb("mv2", [P, JT, 2])
        var1 = sb("var1", [P, JT])
        var2 = sb("var2", [P, JT])
        rstd1 = sb("rstd1", [P, JT])
        rstd2 = sb("rstd2", [P, JT])
        neg1 = sb("neg1", [P, JT])
        shift1 = sb("shift1", [P, JT])
        vin = sb("vin", [P, 2, PAIR])
        ea = sb("ea", [P, PAIR])
        kv = sb("kv", [P, PAIR])
        kva = sb("kva", [P, PAIR])
        past = sb("past", [P, PAIR])
        den = sb("den", [P, PAIR])
        n_hi = sb("n_hi", [P, KT, PAIR], F32R)
        n_lo = sb("n_lo", [P, KT, PAIR], F32R)
        relu = sb("relu", [P, PAIR])
        h_hi = sb("h_hi", [P, 2, PAIR], F32R)
        h_lo = sb("h_lo", [P, 2, PAIR], F32R)

        turn = [psum("turn0"), psum("turn1")]
        y1 = [psum("y1_0"), psum("y1_1")]
        acc = [psum(f"acc{t}") for t in range(JT)]

        par_in = sem("par_in")
        scale_in = sem("scale_in")
        lora_in = sem("lora_in")
        bias_up_in = sem("bias_up_in")
        bias_dn_in = sem("bias_dn_in")
        qup_in = [sem(f"qup_in{s}") for s in range(2)]
        qdn_in = [sem(f"qdn_in{s}") for s in range(2)]
        col_in = [sem(f"col_in{s}") for s in range(2)]
        x_mix = [sem(f"x_mix{j}") for j in range(JT)]
        x_in = [sem(f"x_in{j}") for j in range(JT)]
        v_in = [sem(f"v_in{s}") for s in range(2)]
        stored = [sem(f"stored{j}") for j in range(JT)]
        const_set = sem("const_set")
        id_zero = sem("id_zero")
        id_done = sem("id_done")
        par_step = sem("par_step")
        par_done = sem("par_done")
        deq_done = sem("deq_done")
        wt_done = sem("wt_done")
        whi_done = sem("whi_done")
        wlo_done = sem("wlo_done")
        bn1_done = sem("bn1_done")
        mv1_done = sem("mv1_done")
        stats_there = sem("stats_there")
        ln1_step = sem("ln1_step")
        ln1_done = sem("ln1_done")
        e_done = sem("e_done")
        et_done = sem("et_done")
        ea_done = sem("ea_done")
        kv_done = sem("kv_done")
        kva_done = sem("kva_done")
        pastb_done = sem("pastb_done")
        den_done = sem("den_done")
        rec_done = sem("rec_done")
        pasta_done = sem("pasta_done")
        num_done = sem("num_done")
        wkv_done = sem("wkv_done")
        yt_done = sem("yt_done")
        x1_done = sem("x1_done")
        bn2_done = sem("bn2_done")
        mv2_done = sem("mv2_done")
        ln2_step = sem("ln2_step")
        ln2_done = sem("ln2_done")
        n_done = sem("n_done")
        nt_done = sem("nt_done")
        nhi_done = sem("nhi_done")
        nlo_done = sem("nlo_done")
        up_done = sem("up_done")
        relu_done = sem("relu_done")
        hhi_done = sem("hhi_done")
        hlo_done = sem("hlo_done")
        down_done = sem("down_done")
        acc_done = sem("acc_done")
        res_done = sem("res_done")
        out_done = sem("out_done")

        block = ctx.enter_context(nc.Block())

        @block.sync
        def _(sp):
            def load_weights(i):
                if i >= 2:
                    sp.wait_ge(wt_done, 2 * (i - 1))
                sp.dma_start(wq_up[:, i % 2, :].bitcast(I32), q_up[i]).then_inc(qup_in[i % 2], 16)
                sp.dma_start(wq_dn[:, i % 2, :].bitcast(I32), q_dn[i]).then_inc(qdn_in[i % 2], 16)
                sp.dma_start(lo_cols[:, i % 2, :], lora_cols[i]).then_inc(col_in[i % 2], 16)

            def load_mix(q, j):
                sp.dma_start(mix[:, j, :], xt[q, j]).then_inc(x_mix[j], 16)

            def load_x(q, j):
                sp.dma_start(xin[:, j, :], xt[q, j]).then_inc(x_in[j], 16)

            def load_v(q, c):
                sp.dma_start(vin[:, c % 2, :], vt[q, c]).then_inc(v_in[c % 2], 16)

            for j in range(JT):
                load_mix(0, j)
            sp.dma_start(par[:, 0, :], decay).then_inc(par_in, 16)
            sp.dma_start(par[:, 1, :], first).then_inc(par_in, 16)
            load_v(0, 0)
            load_v(0, 1)
            sp.dma_start(sc_up[:], s_up).then_inc(scale_in, 16)
            sp.dma_start(sc_dn[:], s_dn).then_inc(scale_in, 16)
            sp.dma_start(lo_rows[:], lora_rows).then_inc(lora_in, 16)
            load_weights(0)
            load_weights(1)
            sp.dma_start(bias_up[:], b_up).then_inc(bias_up_in, 16)
            sp.dma_start(bias_dn[:], b_dn.broadcast_to([P, D])).then_inc(bias_dn_in, 16)
            for j in range(JT):
                load_x(0, j)
            for i in range(2, HT):
                if i < KT:
                    sp.wait_ge(kv_done, i - 1)
                    load_v(0, i)
                load_weights(i)

            def pair(p, is_first, is_last):
                if not is_last:
                    q = p + 1
                    sp.wait_ge(nt_done, KT * q)
                    for j in range(JT):
                        load_mix(q, j)
                    sp.wait_ge(kv_done, KT * q)
                    load_v(q, 0)
                    load_v(q, 1)
                if not is_first:
                    for j in range(JT):
                        sp.wait_ge(out_done, JT * p - JT + j + 1)
                        sp.dma_start(ot[p - 1, j], res[:, j, :]).then_inc(stored[j], 16)
                if not is_last:
                    for j in range(JT):
                        sp.wait_ge(res_done, JT * p + j + 1)
                        load_x(q, j)
                    for c in range(2, KT):
                        sp.wait_ge(kv_done, KT * q + c - 1)
                        load_v(q, c)

            pair(0, True, False)
            with sp.Fori(1, NPAIR - 1) as p:
                pair(p, False, False)
            pair(NPAIR - 1, False, True)
            for j in range(JT):
                sp.wait_ge(out_done, JT * (NPAIR - 1) + j + 1)
                sp.dma_start(ot[NPAIR - 1, j], res[:, j, :]).then_inc(stored[j], 16)
            for j in range(JT):
                sp.wait_ge(stored[j], 16 * NPAIR)

        @block.gpsimd
        def _(pool):
            nc.gpsimd.memset(ident[:], 0.0).then_inc(id_zero, 1)
            nc.gpsimd.memset(base[:], 2.718281828459045).then_inc(const_set, 1)
            nc.gpsimd.memset(half[:], -0.5).then_inc(const_set, 1)
            nc.gpsimd.memset(eps[:], EPS).then_inc(const_set, 1)
            pool.wait_ge(id_zero, 1)
            nc.gpsimd.affine_select(out=ident[:], in_=ident[:], compare_op=ALU.not_equal, fill=1.0, base=0,
                                    pattern=[[-1, P]], channel_multiplier=1).then_inc(id_done, 1)
            pool.wait_ge(par_in, 32)
            pool.wait_ge(const_set, 3)
            nc.gpsimd.tensor_tensor(expo[:, 0, :], base[:], par[:, 0, :], ALU.pow).then_inc(par_step, 1)
            nc.gpsimd.tensor_scalar(expo[:, 1, :], par[:, 1, :], 0.0, -1.0, ALU.max, ALU.mult).then_inc(par_step, 1)
            nc.gpsimd.tensor_scalar(expo[:, 2, :], par[:, 1, :], 0.0, None, ALU.min).then_inc(par_step, 1)
            pool.wait_ge(par_step, 3)
            nc.gpsimd.tensor_scalar(expo[:, 0, :], expo[:, 0, :], -1.0, None, ALU.mult).then_inc(par_step, 1)
            nc.gpsimd.tensor_tensor(alpha[:], base[:], expo[:, 1, :], ALU.pow).then_inc(par_done, 1)
            nc.gpsimd.tensor_tensor(beta[:], base[:], expo[:, 2, :], ALU.pow).then_inc(par_done, 1)
            pool.wait_ge(par_step, 4)
            nc.gpsimd.tensor_tensor(omega[:], base[:], expo[:, 0, :], ALU.pow).then_inc(par_done, 1)

            def ln1(q):
                pool.wait_ge(mv1_done, JT * q + JT)
                nc.gpsimd.tensor_tensor(var1[:], mv1[:, :, 1], eps[:], ALU.add).then_inc(ln1_step, 1)
                nc.gpsimd.tensor_scalar(neg1[:], mv1[:, :, 0], -1.0, None, ALU.mult).then_inc(ln1_step, 1)
                pool.wait_ge(ln1_step, 3 * q + 2)
                nc.gpsimd.tensor_tensor(rstd1[:], var1[:], half[:], ALU.pow).then_inc(ln1_step, 1)
                pool.wait_ge(ln1_step, 3 * q + 3)
                nc.gpsimd.tensor_tensor(shift1[:], neg1[:], rstd1[:], ALU.mult).then_inc(ln1_done, 1)

            def ln2(q):
                pool.wait_ge(mv2_done, JT * q + JT)
                nc.gpsimd.tensor_tensor(var2[:], mv2[:, :, 1], eps[:], ALU.add).then_inc(ln2_step, 1)
                pool.wait_ge(ln2_step, q + 1)
                nc.gpsimd.tensor_tensor(rstd2[:], var2[:], half[:], ALU.pow).then_inc(ln2_done, 1)

            def wkv(q, c):
                pool.wait_ge(num_done, KT * q + c + 1)
                y = mix[:, :, c * P:(c + 1) * P]
                nc.gpsimd.tensor_tensor(y, y, den[:].rearrange("p (j t) -> p j t", t=P),
                                        ALU.mult).then_inc(wkv_done, 1)

            def residual(p, j, is_first):
                if not is_first:
                    pool.wait_ge(stored[j], 16 * p)
                nc.gpsimd.tensor_tensor(res[:, j, :], xin[:, j, :], bias_dn[:], ALU.add).then_inc(res_done, 1)

            def hidden_lo(p, i, is_first):
                pool.wait_ge(hhi_done, HT * p + i + 1)
                if not is_first or i >= 2:
                    pool.wait_ge(down_done, HT * p + i - 1)
                nc.gpsimd.tensor_tensor(h_lo[:, i % 2, :], relu[:], h_hi[:, i % 2, :].bitcast(F32),
                                        ALU.subtract).then_inc(hlo_done, 1)

            ln1(0)
            for c in range(KT):
                wkv(0, c)
            ln2(0)
            pool.wait_ge(bias_dn_in, 16)

            def pair(p, is_first, is_last):
                for i in range(HT):
                    hidden_lo(p, i, is_first)
                    if i in (2, 3):
                        residual(p, 2 * (i - 2), is_first)
                        residual(p, 2 * (i - 2) + 1, is_first)
                    if is_last:
                        continue
                    q = p + 1
                    if i == 0:
                        ln1(q)
                    if i in (4, 5, 7, 8):
                        wkv(q, (4, 5, 7, 8).index(i))
                    if i == 12:
                        ln2(q)

            pair(0, True, False)
            with pool.Fori(1, NPAIR - 1) as p:
                pair(p, False, False)
            pair(NPAIR - 1, False, True)

        @block.scalar
        def _(act):
            def weight_hi(i):
                act.wait_ge(wt_done, 2 * i + 1)
                nc.scalar.activation(up_hi[:, :, i * P:(i + 1) * P],
                                     y1[0][:].rearrange("p (k h) -> p k h", h=P), ACT.Copy).then_inc(whi_done, 1)
                act.wait_ge(wt_done, 2 * i + 2)
                nc.scalar.activation(dn_hi[:, i, :], y1[1][:], ACT.Copy).then_inc(whi_done, 1)

            def exp_k(q, j):
                nc.scalar.activation(mix[:, j, :], mix[:, j, :], ACT.Exp, bias=shift1[:, j:j + 1],
                                     scale=rstd1[:, j:j + 1]).then_inc(e_done, 1)

            def exp_scaled(q, c, is_first):
                act.wait_ge(et_done, KT * q + c + 1)
                if not is_first or c >= 1:
                    act.wait_ge(pastb_done, 3 * (KT * q + c))
                nc.scalar.activation(ea[:], turn[c % 2][:], ACT.Copy, scale=alpha[:, c:c + 1]).then_inc(ea_done, 1)

            def kv_scaled(q, c, is_first):
                act.wait_ge(kv_done, KT * q + c + 1)
                if not is_first or c >= 1:
                    act.wait_ge(pasta_done, 3 * (KT * q + c))
                nc.scalar.activation(kva[:], kv[:], ACT.Copy, scale=alpha[:, c:c + 1]).then_inc(kva_done, 1)

            def norm_hi(q, k):
                act.wait_ge(nt_done, KT * q + k + 1)
                nc.scalar.activation(n_hi[:, k, :], turn[k % 2][:], ACT.Copy).then_inc(nhi_done, 1)

            def hidden(p, i, is_first):
                act.wait_ge(up_done, HT * p + i + 1)
                if not is_first or i >= 1:
                    act.wait_ge(hlo_done, HT * p + i)
                nc.scalar.activation(relu[:], y1[i % 2][:], ACT.Relu, bias=bias_up[:, i:i + 1]).then_inc(relu_done, 1)
                if not is_first or i >= 2:
                    act.wait_ge(down_done, HT * p + i - 1)
                act.wait_ge(relu_done, HT * p + i + 1)
                nc.scalar.activation(h_hi[:, i % 2, :], relu[:], ACT.Copy).then_inc(hhi_done, 1)

            act.wait_ge(ln1_done, 1)
            for j in range(JT):
                exp_k(0, j)
            act.wait_ge(par_done, 3)
            for i in range(HT):
                if i < KT:
                    exp_scaled(0, i, True)
                    kv_scaled(0, i, True)
                weight_hi(i)
            for k in range(KT):
                norm_hi(0, k)
            act.wait_ge(bias_up_in, 16)

            def pair(p, is_first, is_last):
                for i in range(HT):
                    hidden(p, i, is_first)
                    if is_last:
                        continue
                    q = p + 1
                    if i == 1:
                        act.wait_ge(ln1_done, q + 1)
                        for j in range(JT):
                            exp_k(q, j)
                    if 4 <= i < 4 + KT:
                        kv_scaled(q, i - 4, False)
                    if 3 <= i < 3 + KT:
                        exp_scaled(q, i - 3, False)
                if not is_last:
                    for k in range(KT):
                        norm_hi(q, k)

            pair(0, True, False)
            with act.Fori(1, NPAIR - 1) as p:
                pair(p, False, False)
            pair(NPAIR - 1, False, True)

        @block.vector
        def _(dve):
            def dequantise(i):
                up = wq_up[:, i % 2, :].rearrange("p (b e) -> p b e", e=BLOCK)
                dn = wq_dn[:, i % 2, :].rearrange("p (b e) -> p b e", e=BLOCK)
                dve.wait_ge(qup_in[i % 2], 16 * (i // 2 + 1))
                nc.vector.scalar_tensor_tensor(out=up, in0=up.bitcast(I32), scalar=-ZERO,
                                               in1=sc_up[:, i, :, None].broadcast_to([P, NB, BLOCK]),
                                               op0=ALU.add, op1=ALU.mult).then_inc(deq_done, 1)
                dve.wait_ge(qdn_in[i % 2], 16 * (i // 2 + 1))
                nc.vector.scalar_tensor_tensor(out=dn, in0=dn.bitcast(I32), scalar=-ZERO,
                                               in1=sc_dn[:, i, :, None].broadcast_to([P, DB, BLOCK]),
                                               op0=ALU.add, op1=ALU.mult).then_inc(deq_done, 1)

            def weight_lo(i):
                hi = up_hi[:, :, i * P:(i + 1) * P]
                dve.wait_ge(whi_done, 2 * i + 1)
                nc.vector.tensor_tensor(up_lo[:, :, i * P:(i + 1) * P], y1[0][:].rearrange("p (k h) -> p k h", h=P),
                                        hi.bitcast(F32), ALU.subtract).then_inc(wlo_done, 1)
                dve.wait_ge(whi_done, 2 * i + 2)
                nc.vector.tensor_tensor(dn_lo[:, i, :], y1[1][:], dn_hi[:, i, :].bitcast(F32),
                                        ALU.subtract).then_inc(wlo_done, 1)

            def stats1(q):
                for j in range(JT):
                    dve.wait_ge(x_mix[j], 16 * q + 16)
                    nc.vector.bn_stats(st1[:, j, :], mix[:, j, :]).then_inc(bn1_done, 1)
                dve.wait_ge(bn1_done, JT * q + JT)
                dve.sem_inc(stats_there, 1)
                for j in range(JT):
                    nc.vector.bn_aggr(mv1[:, j, :], st1[:, j, :]).then_inc(mv1_done, 1)

            def scan(state, step, c, done):
                for s in range(2):
                    a = s * SEQ
                    nc.vector.tensor_tensor_scan(state[:, a + 1:a + SEQ],
                                                 omega[:, c:c + 1].broadcast_to([P, SEQ - 1]),
                                                 step[:, a:a + SEQ - 1], 0.0, ALU.mult, ALU.add).then_inc(done, 1)
                nc.vector.tensor_copy(state[:, 0:PAIR:SEQ], step[:, 0:PAIR:SEQ]).then_inc(done, 1)

            def recurrence(q, c, is_first):
                e_t = turn[c % 2]
                done = KT * q + c
                dve.wait_ge(ea_done, done + 1)
                dve.wait_ge(v_in[c % 2], 32 * q + 16 * (c // 2 + 1))
                if not is_first or c >= 1:
                    dve.wait_ge(num_done, done)
                nc.vector.tensor_tensor(kv[:], e_t[:], vin[:, c % 2, :], ALU.mult).then_inc(kv_done, 1)
                scan(past, ea, c, pastb_done)
                if not is_first or c >= 1:
                    dve.wait_ge(wkv_done, done)
                dve.wait_ge(pastb_done, 3 * done + 3)
                nc.vector.scalar_tensor_tensor(out=den[:], in0=e_t[:], scalar=beta[:, c:c + 1], in1=past[:],
                                               op0=ALU.mult, op1=ALU.add).then_inc(den_done, 1)
                dve.wait_ge(den_done, done + 1)
                nc.vector.reciprocal(den[:], den[:]).then_inc(rec_done, 1)
                dve.wait_ge(kva_done, done + 1)
                scan(past, kva, c, pasta_done)
                dve.wait_ge(pasta_done, 3 * done + 3)
                nc.vector.scalar_tensor_tensor(out=mix[:, :, c * P:(c + 1) * P],
                                               in0=kv[:].rearrange("p (j t) -> p j t", t=P),
                                               scalar=beta[:, c:c + 1],
                                               in1=past[:].rearrange("p (j t) -> p j t", t=P),
                                               op0=ALU.mult, op1=ALU.add).then_inc(num_done, 1)

            def add_x(q, j):
                dve.wait_ge(x_in[j], 16 * q + 16)
                dve.wait_ge(yt_done, JT * q + j + 1)
                nc.vector.tensor_tensor(xin[:, j, :], turn[j % 2][:], xin[:, j, :], ALU.add).then_inc(x1_done, 1)

            def stats2(q, j):
                dve.wait_ge(x1_done, JT * q + j + 1)
                nc.vector.bn_stats(st2[:, j, :], xin[:, j, :]).then_inc(bn2_done, 1)

            def norm(q):
                for j in (0, 2):
                    add_x(q, j)
                    add_x(q, j + 1)
                    stats2(q, j)
                    stats2(q, j + 1)
                dve.wait_ge(bn2_done, JT * q + JT)
                dve.sem_inc(stats_there, 1)
                for j in range(JT):
                    nc.vector.bn_aggr(mv2[:, j, :], st2[:, j, :]).then_inc(mv2_done, 1)
                dve.wait_ge(ln2_done, q + 1)
                for j in range(JT):
                    nc.vector.tensor_scalar(mix[:, j, :], xin[:, j, :], mv2[:, j, 0:1], rstd2[:, j:j + 1],
                                            ALU.subtract, ALU.mult).then_inc(n_done, 1)

            def norm_lo(q, k):
                dve.wait_ge(nhi_done, KT * q + k + 1)
                nc.vector.tensor_tensor(n_lo[:, k, :], turn[k % 2][:], n_hi[:, k, :].bitcast(F32),
                                        ALU.subtract).then_inc(nlo_done, 1)

            def output(p, t):
                dve.wait_ge(res_done, JT * p + t + 1)
                if t < JT - 1:
                    dve.wait_ge(acc_done, (JT - 1) * p + t + 1)
                else:
                    dve.wait_ge(down_done, HT * p + HT)
                nc.vector.tensor_tensor(res[:, t, :], acc[t][:], res[:, t, :], ALU.add).then_inc(out_done, 1)

            stats1(0)
            dve.wait_ge(scale_in, 32)
            dequantise(0)
            dequantise(1)
            dve.wait_ge(par_done, 3)
            for i in range(HT):
                if i < KT:
                    recurrence(0, i, True)
                if i == KT + 1:
                    norm(0)
                weight_lo(i)
                if i + 2 < HT:
                    dve.wait_ge(wt_done, 2 * i + 2)
                    dequantise(i + 2)
            for k in range(KT):
                norm_lo(0, k)

            def pair(p, is_last):
                if not is_last:
                    q = p + 1
                    stats1(q)
                    for c in range(KT):
                        recurrence(q, c, False)
                    norm(q)
                    for k in range(KT):
                        norm_lo(q, k)
                for t in range(JT):
                    output(p, t)

            pair(0, False)
            with dve.Fori(1, NPAIR - 1) as p:
                pair(p, False)
            pair(NPAIR - 1, True)

        @block.tensor
        def _(pe):
            def weights(i):
                cols = lo_cols[:, i % 2, :]
                pe.wait_ge(deq_done, 2 * i + 2)
                pe.wait_ge(col_in[i % 2], 16 * (i // 2 + 1))
                if i >= 1:
                    pe.wait_ge(wlo_done, 2 * i - 1)
                for k in range(KT):
                    nc.tensor.matmul(y1[0][:, k * P:(k + 1) * P], wq_up[:, i % 2, k * P:(k + 1) * P], ident[:],
                                     start=(k == 0), stop=False, is_transpose=True, skip_group_check=True)
                for k in range(KT):
                    last = nc.tensor.matmul(y1[0][:, k * P:(k + 1) * P], lo_rows[0:RANK, k * P:(k + 1) * P],
                                            cols[0:RANK, :], start=False, stop=(k == KT - 1), skip_group_check=True)
                last.then_inc(wt_done, 1)
                if i >= 1:
                    pe.wait_ge(wlo_done, 2 * i)
                for k in range(KT):
                    nc.tensor.matmul(y1[1][:, k * P:(k + 1) * P], wq_dn[:, i % 2, k * P:(k + 1) * P], ident[:],
                                     start=(k == 0), stop=False, is_transpose=True, skip_group_check=True)
                nc.tensor.matmul(y1[1][:], cols[LORA_DN:LORA_DN + RANK, :], lo_rows[LORA_DN:LORA_DN + RANK, :],
                                 start=False, stop=True, skip_group_check=True).then_inc(wt_done, 1)

            def turn_e(q, c, is_first):
                if c == 0:
                    pe.wait_ge(e_done, JT * q + JT)
                if c >= 2:
                    pe.wait_ge(den_done, KT * q + c - 1)
                elif not is_first:
                    pe.wait_ge(nlo_done, KT * q - 1 + c)
                for j in range(JT):
                    last = nc.tensor.transpose(turn[c % 2][:, j * P:(j + 1) * P], mix[:, j, c * P:(c + 1) * P], ident[:])
                last.then_inc(et_done, 1)

            def turn_y(q, j):
                if j == 0:
                    pe.wait_ge(wkv_done, KT * q + KT)
                if j >= 2:
                    pe.wait_ge(x1_done, JT * q + j - 1)
                else:
                    pe.wait_ge(den_done, KT * q + 3 + j)
                for c in range(KT):
                    last = nc.tensor.transpose(turn[j % 2][:, c * P:(c + 1) * P], mix[:, j, c * P:(c + 1) * P], ident[:])
                last.then_inc(yt_done, 1)

            def turn_n(q, k):
                if k == 0:
                    pe.wait_ge(n_done, JT * q + JT)
                if k >= 2:
                    pe.wait_ge(nlo_done, KT * q + k - 1)
                for j in range(JT):
                    last = nc.tensor.transpose(turn[k % 2][:, j * P:(j + 1) * P], mix[:, j, k * P:(k + 1) * P], ident[:])
                last.then_inc(nt_done, 1)

            def up(p, i, is_first):
                if i == 0:
                    pe.wait_ge(nlo_done, KT * p + KT)
                if not is_first or i >= 2:
                    pe.wait_ge(relu_done, HT * p + i - 1)
                cols = slice(i * P, (i + 1) * P)
                for k in range(KT):
                    nc.tensor.matmul(y1[i % 2][:], up_hi[:, k, cols], n_hi[:, k, :], start=(k == 0), stop=False)
                    nc.tensor.matmul(y1[i % 2][:], up_hi[:, k, cols], n_lo[:, k, :], start=False, stop=False)
                    last = nc.tensor.matmul(y1[i % 2][:], up_lo[:, k, cols], n_hi[:, k, :], start=False,
                                            stop=(k == KT - 1))
                last.then_inc(up_done, 1)

            def down(p, i, is_first):
                pe.wait_ge(hlo_done, HT * p + i + 1)
                for t in range(JT):
                    if i == 0 and not is_first:
                        pe.wait_ge(out_done, JT * p - JT + t + 1)
                    rows = slice(t * P, (t + 1) * P)
                    hi, lo = h_hi[:, i % 2, rows], h_lo[:, i % 2, rows]
                    nc.tensor.matmul(acc[t][:], hi, dn_hi[:, i, :], start=(i == 0), stop=False)
                    nc.tensor.matmul(acc[t][:], hi, dn_lo[:, i, :], start=False, stop=False)
                    last = nc.tensor.matmul(acc[t][:], lo, dn_hi[:, i, :], start=False, stop=(i == HT - 1))
                    if i == HT - 1 and t < JT - 1:
                        last.then_inc(acc_done, 1)
                last.then_inc(down_done, 1)

            pe.wait_ge(id_done, 1)
            pe.wait_ge(lora_in, 16)
            for i in range(HT):
                if i < KT:
                    turn_e(0, i, True)
                if i == KT + 1:
                    for j in range(JT):
                        turn_y(0, j)
                weights(i)
            for k in range(KT):
                turn_n(0, k)
            pe.wait_ge(wlo_done, 2 * HT)

            def pair(p, is_first, is_last):
                q = p + 1
                for i in range(HT):
                    if i == HT - 1 and not is_last:
                        turn_n(q, 0)
                        turn_n(q, 1)
                    up(p, i, is_first)
                    if not is_last and 3 <= i < 3 + KT:
                        turn_e(q, i - 3, False)
                    if not is_last and i in (10, 11):
                        turn_y(q, 2 * (i - 10))
                        turn_y(q, 2 * (i - 10) + 1)
                    if i >= 1:
                        down(p, i - 1, is_first)
                if not is_last:
                    turn_n(q, 2)
                    turn_n(q, 3)
                down(p, HT - 1, is_first)

            pair(0, True, False)
            with pe.Fori(1, NPAIR - 1) as p:
                pair(p, False, False)
            pair(NPAIR - 1, False, True)


def kernel(x, ctx_2048, L0_xattn_time_decay, L0_xattn_time_first, L0_ffn_w_up_q, L0_ffn_w_up_scale,
           L0_ffn_b_up, L0_ffn_w_up_lora_a, L0_ffn_w_up_lora_b, L0_ffn_w_down_q, L0_ffn_w_down_scale,
           L0_ffn_b_down, L0_ffn_w_down_lora_a, L0_ffn_w_down_lora_b):
    import numpy as np
    import concourse.bacc as bacc
    from concourse.bass_utils import run_bass_kernel_spmd

    def lay(a):
        return np.ascontiguousarray(a)

    gap = np.zeros((LORA_DN - RANK, 1), np.float32)
    a_up, b_up_l = np.asarray(L0_ffn_w_up_lora_a), np.asarray(L0_ffn_w_up_lora_b)
    a_dn, b_dn_l = np.asarray(L0_ffn_w_down_lora_a), np.asarray(L0_ffn_w_down_lora_b)
    rows = np.concatenate([a_up.T, gap.repeat(D, 1), b_dn_l])
    cols = np.concatenate([b_up_l, gap.repeat(HID, 1), a_dn.T])
    arrays = {
        "x": lay(np.asarray(x).reshape(BATCH * SEQ, D)),
        "ctx_t": lay(np.asarray(ctx_2048).transpose(2, 0, 1).reshape(D, BATCH * SEQ)),
        "decay": lay(np.asarray(L0_xattn_time_decay).reshape(KT, P).T),
        "first": lay(np.asarray(L0_xattn_time_first).reshape(KT, P).T),
        "q_up": lay(np.asarray(L0_ffn_w_up_q).reshape(HT, P, D)),
        "s_up": lay(np.asarray(L0_ffn_w_up_scale).reshape(HT, P, NB).transpose(1, 0, 2)),
        "b_up": lay(np.asarray(L0_ffn_b_up).reshape(HT, P).T),
        "lora_rows": lay(rows),
        "lora_cols": lay(cols.reshape(LORA_DN + RANK, HT, P).transpose(1, 0, 2)),
        "q_dn": lay(np.asarray(L0_ffn_w_down_q).reshape(KT, P, HT, P).transpose(2, 1, 0, 3).reshape(HT, P, D)),
        "s_dn": lay(np.asarray(L0_ffn_w_down_scale).reshape(KT, P, HT, P // BLOCK)
                    .transpose(1, 2, 0, 3).reshape(P, HT, DB)),
        "b_dn": lay(np.asarray(L0_ffn_b_down).reshape(1, D)),
    }
    nc = bacc.Bacc("TRN2", target_bir_lowering=False, num_devices=1)
    args = [nc.dram_tensor(f"in_{n}", a.shape, mybir.dt.from_np(a.dtype), kind="ExternalInput").ap()
            for n, a in arrays.items()]
    out = nc.dram_tensor("out", (BATCH * SEQ, D), F32, kind="ExternalOutput").ap()
    build(nc, *args, out)
    done = run_bass_kernel_spmd(nc, [{f"in_{n}": a for n, a in arrays.items()}], core_ids=[0])
    return done.results[0]["out"].reshape(BATCH, SEQ, D)
```

```python
from contextlib import ExitStack

import concourse.bass as bass
from concourse import mybir

F32 = mybir.dt.float32
F32R = mybir.dt.float32r
I32 = mybir.dt.int32
ALU = mybir.AluOpType
ACT = mybir.ActivationFunctionType

P = 128
BATCH = 16
SEQ = 256
D = 512
HID = 2048
RANK = 16
BLOCK = 64
ZERO = 7.5
EPS = 1e-5
PAIR = 2 * SEQ
NPAIR = BATCH * SEQ // PAIR
KT = D // P
HT = HID // P
JT = PAIR // P
NB = D // BLOCK
DB = KT * (P // BLOCK)
LORA = 3 * RANK
LORA_DN = 64
LORA_ROWS = LORA_DN + LORA

EARLY = 14
BY_DVE = 4


def weight_tiles(step):
    n = EARLY + step + min(max(step - 9, 0), 3)
    if 9 <= step < 12:
        return [n], [n + 1]
    return [], [n] if n < 2 * HT else []
BN = 6


def build(nc, x, ctx_t, decay, first, q_up, q_dn, w_scales, b_up, b_dn, lora_rows, lora_cols, out):
    xt = x.rearrange("(n j p) d -> n j p d", p=P, j=JT)
    ot = out.rearrange("(n j p) d -> n j p d", p=P, j=JT)
    vt = ctx_t.rearrange("(c p) (n t) -> n c p t", p=P, t=PAIR)

    with ExitStack() as ctx:
        def sb(name, shape, dt=F32):
            return ctx.enter_context(nc.sbuf_tensor(name, shape, dt))

        def psum(name):
            return ctx.enter_context(nc.psum_tensor(name, [P, 512], F32))

        def sem(name):
            return ctx.enter_context(nc.semaphore(name))

        up_hi = sb("up_hi", [P, KT, HID], F32R)
        up_lo = sb("up_lo", [P, KT, HID], F32R)
        dn_hi = sb("dn_hi", [P, HT, D], F32R)
        dn_lo = sb("dn_lo", [P, HT, D], F32R)
        wq_up = sb("wq_up", [P, 2, D])
        wq_dn = sb("wq_dn", [P, 2, D])
        scales = sb("scales", [P, 4, NB + DB])
        rows = sb("rows", [LORA_ROWS, D], F32R)
        cols_raw = sb("cols_raw", [LORA_ROWS, 2, P])
        cols = sb("cols", [LORA_ROWS, 2, P], F32R)
        bias_up = sb("bias_up", [P, HT])
        bias_dn = sb("bias_dn", [P, D])
        ident = sb("ident", [P, P])
        par = sb("par", [P, 2, KT])
        base = sb("base", [P, KT])
        half = sb("half", [P, JT])
        eps = sb("eps", [P, JT])
        expo = sb("expo", [P, 3, KT])
        omega = sb("omega", [P, KT])
        alpha = sb("alpha", [P, KT])
        beta = sb("beta", [P, KT])
        xin = sb("xin", [P, JT, D])
        mix = sb("mix", [P, JT, D])
        res = sb("res", [P, JT, D])
        rows_raw = res[0:LORA_ROWS, 0, :]
        st1 = sb("st1", [P, JT, BN])
        st2 = sb("st2", [P, JT, BN])
        mv1 = sb("mv1", [P, JT, 2])
        mv2 = sb("mv2", [P, JT, 2])
        var1 = sb("var1", [P, JT])
        var2 = sb("var2", [P, JT])
        rstd1 = sb("rstd1", [P, JT])
        rstd2 = sb("rstd2", [P, JT])
        neg1 = sb("neg1", [P, JT])
        shift1 = sb("shift1", [P, JT])
        vin = sb("vin", [P, 2, PAIR])
        ea = sb("ea", [P, PAIR])
        kv = sb("kv", [P, PAIR])
        kva = sb("kva", [P, PAIR])
        past = sb("past", [P, PAIR])
        den = sb("den", [P, PAIR])
        n_hi = sb("n_hi", [P, KT, PAIR], F32R)
        n_lo = sb("n_lo", [P, KT, PAIR], F32R)
        relu = sb("relu", [P, PAIR])
        h_hi = sb("h_hi", [P, 2, PAIR], F32R)
        h_lo = sb("h_lo", [P, 2, PAIR], F32R)

        turn = [psum("turn0"), psum("turn1")]
        y1 = [psum("y1_0"), psum("y1_1")]
        acc = [psum(f"acc{t}") for t in range(JT)]

        par_in = sem("par_in")
        lora_in = sem("lora_in")
        bias_up_in = sem("bias_up_in")
        bias_dn_in = sem("bias_dn_in")
        qup_in = [sem(f"qup_in{s}") for s in range(2)]
        qdn_in = [sem(f"qdn_in{s}") for s in range(2)]
        scale_in = [sem(f"scale_in{s}") for s in range(4)]
        col_in = [sem(f"col_in{s}") for s in range(2)]
        x_mix = [sem(f"x_mix{j}") for j in range(JT)]
        x_in = [sem(f"x_in{j}") for j in range(JT)]
        v_in = [sem(f"v_in{s}") for s in range(2)]
        stored = [sem(f"stored{j}") for j in range(JT)]
        const_set = sem("const_set")
        id_zero = sem("id_zero")
        id_done = sem("id_done")
        par_step = sem("par_step")
        par_done = sem("par_done")
        rows_hi = sem("rows_hi")
        rows_lo = sem("rows_lo")
        rows_done = sem("rows_done")
        cols_hi = sem("cols_hi")
        cols_done = sem("cols_done")
        deq_done = sem("deq_done")
        centred = sem("centred")
        pool_deq_done = sem("pool_deq_done")
        wt_done = sem("wt_done")
        full_done = sem("full_done")
        whi_done = sem("whi_done")
        wlo_done = sem("wlo_done")
        bn1_done = sem("bn1_done")
        mv1_done = sem("mv1_done")
        stats_there = sem("stats_there")
        ln1_step = sem("ln1_step")
        ln1_done = sem("ln1_done")
        e_done = sem("e_done")
        et_done = sem("et_done")
        ea_done = sem("ea_done")
        kv_done = sem("kv_done")
        kva_done = sem("kva_done")
        pastb_done = sem("pastb_done")
        den_done = sem("den_done")
        rec_done = sem("rec_done")
        pasta_done = sem("pasta_done")
        num_done = sem("num_done")
        wkv_done = sem("wkv_done")
        yt_done = sem("yt_done")
        x1_done = sem("x1_done")
        bn2_done = sem("bn2_done")
        mv2_done = sem("mv2_done")
        ln2_step = sem("ln2_step")
        ln2_done = sem("ln2_done")
        n_done = sem("n_done")
        nt_done = sem("nt_done")
        nhi_done = sem("nhi_done")
        nlo_done = sem("nlo_done")
        up_done = sem("up_done")
        relu_done = sem("relu_done")
        hhi_done = sem("hhi_done")
        hlo_done = sem("hlo_done")
        down_done = sem("down_done")
        acc_done = sem("acc_done")
        res_done = sem("res_done")
        out_done = sem("out_done")

        n_bank0 = [turn[0], turn[1], acc[0], acc[1]]
        n_bank = [y1[0], turn[0], turn[1], y1[1]]

        def weight_bank(n):
            return y1[n % 2] if n < EARLY else turn[0]

        block = ctx.enter_context(nc.Block())

        @block.sync
        def _(sp):
            def load_weights(n):
                i = n // 2
                if n >= 4:
                    sp.wait_ge(wlo_done, n - 3)
                if n % 2 == 0:
                    sp.dma_start(scales[:, i % 4, :], w_scales[i]).then_inc(scale_in[i % 4], 16)
                    sp.dma_start(wq_up[:, i % 2, :].bitcast(I32), q_up[i]).then_inc(qup_in[i % 2], 16)
                else:
                    sp.dma_start(wq_dn[:, i % 2, :].bitcast(I32), q_dn[i]).then_inc(qdn_in[i % 2], 16)
                    sp.dma_start(cols_raw[:, i % 2, :], lora_cols[i]).then_inc(col_in[i % 2], 16)

            def load_mix(q, j):
                sp.dma_start(mix[:, j, :], xt[q, j]).then_inc(x_mix[j], 16)

            def load_x(q, j):
                sp.dma_start(xin[:, j, :], xt[q, j]).then_inc(x_in[j], 16)

            def load_v(q, c):
                sp.dma_start(vin[:, c % 2, :], vt[q, c]).then_inc(v_in[c % 2], 16)

            for j in range(JT):
                load_mix(0, j)
            sp.dma_start(par[:, 0, :], decay).then_inc(par_in, 16)
            sp.dma_start(par[:, 1, :], first).then_inc(par_in, 16)
            load_v(0, 0)
            load_v(0, 1)
            sp.dma_start(rows_raw, lora_rows).then_inc(lora_in, 16)
            for n in range(4):
                load_weights(n)
            sp.dma_start(bias_up[:], b_up).then_inc(bias_up_in, 16)
            sp.dma_start(bias_dn[:], b_dn.broadcast_to([P, D])).then_inc(bias_dn_in, 16)
            for j in range(JT):
                load_x(0, j)
            for n in range(4, 8):
                load_weights(n)
            for c in range(2, KT):
                sp.wait_ge(kv_done, c - 1)
                load_v(0, c)
            for n in range(8, EARLY):
                load_weights(n)

            def pair(p, is_first, is_last):
                if not is_last:
                    q = p + 1
                    sp.wait_ge(nt_done, KT * q)
                    for j in range(JT):
                        load_mix(q, j)
                    sp.wait_ge(kv_done, KT * q)
                    load_v(q, 0)
                    load_v(q, 1)
                if not is_first:
                    for j in range(JT):
                        sp.wait_ge(out_done, JT * p - JT + j + 1)
                        sp.dma_start(ot[p - 1, j], res[:, j, :]).then_inc(stored[j], 16)
                if not is_last:
                    if is_first:
                        for n in range(EARLY, EARLY + 6):
                            load_weights(n)
                    for j in range(JT):
                        sp.wait_ge(res_done, JT * p + j + 1)
                        load_x(q, j)
                    for c in range(2, KT):
                        if is_first:
                            load_weights(EARLY + 2 + 2 * c)
                            load_weights(EARLY + 3 + 2 * c)
                        sp.wait_ge(kv_done, KT * q + c - 1)
                        load_v(q, c)
                    if is_first:
                        for n in range(EARLY + 2 + 2 * KT, 2 * HT):
                            load_weights(n)

            pair(0, True, False)
            with sp.Fori(1, NPAIR - 1) as p:
                pair(p, False, False)
            pair(NPAIR - 1, False, True)
            for j in range(JT):
                sp.wait_ge(out_done, JT * (NPAIR - 1) + j + 1)
                sp.dma_start(ot[NPAIR - 1, j], res[:, j, :]).then_inc(stored[j], 16)
            for j in range(JT):
                sp.wait_ge(stored[j], 16 * NPAIR)

        @block.gpsimd
        def _(pool):
            nc.gpsimd.memset(ident[:], 0.0).then_inc(id_zero, 1)
            nc.gpsimd.memset(base[:], 2.718281828459045).then_inc(const_set, 1)
            nc.gpsimd.memset(half[:], -0.5).then_inc(const_set, 1)
            nc.gpsimd.memset(eps[:], EPS).then_inc(const_set, 1)
            pool.wait_ge(id_zero, 1)
            nc.gpsimd.affine_select(out=ident[:], in_=ident[:], compare_op=ALU.not_equal, fill=1.0, base=0,
                                    pattern=[[-1, P]], channel_multiplier=1).then_inc(id_done, 1)
            def ln1(q):
                pool.wait_ge(mv1_done, JT * q + JT)
                nc.gpsimd.tensor_tensor(var1[:], mv1[:, :, 1], eps[:], ALU.add).then_inc(ln1_step, 1)
                nc.gpsimd.tensor_scalar(neg1[:], mv1[:, :, 0], -1.0, None, ALU.mult).then_inc(ln1_step, 1)
                pool.wait_ge(ln1_step, 3 * q + 2)
                nc.gpsimd.tensor_tensor(rstd1[:], var1[:], half[:], ALU.pow).then_inc(ln1_step, 1)
                pool.wait_ge(ln1_step, 3 * q + 3)
                nc.gpsimd.tensor_tensor(shift1[:], neg1[:], rstd1[:], ALU.mult).then_inc(ln1_done, 1)

            def ln2(q):
                pool.wait_ge(mv2_done, JT * q + JT)
                nc.gpsimd.tensor_tensor(var2[:], mv2[:, :, 1], eps[:], ALU.add).then_inc(ln2_step, 1)
                pool.wait_ge(ln2_step, q + 1)
                nc.gpsimd.tensor_tensor(rstd2[:], var2[:], half[:], ALU.pow).then_inc(ln2_done, 1)

            def wkv(q, c):
                pool.wait_ge(num_done, KT * q + c + 1)
                y = mix[:, :, c * P:(c + 1) * P]
                nc.gpsimd.tensor_tensor(y, y, den[:].rearrange("p (j t) -> p j t", t=P),
                                        ALU.mult).then_inc(wkv_done, 1)

            def residual(p, j, is_first):
                if not is_first:
                    pool.wait_ge(stored[j], 16 * p)
                nc.gpsimd.tensor_tensor(res[:, j, :], xin[:, j, :], bias_dn[:], ALU.add).then_inc(res_done, 1)

            def hidden_lo(p, i, is_first):
                pool.wait_ge(hhi_done, HT * p + i + 1)
                if not is_first or i >= 2:
                    pool.wait_ge(down_done, HT * p + i - 1)
                nc.gpsimd.tensor_tensor(h_lo[:, i % 2, :], relu[:], h_hi[:, i % 2, :].bitcast(F32),
                                        ALU.subtract).then_inc(hlo_done, 1)

            def weight_lo(n):
                i = n // 2
                pool.wait_ge(whi_done, n + 1)
                if n % 2 == 0:
                    cut = slice(i * P, (i + 1) * P)
                    nc.gpsimd.tensor_tensor(up_lo[:, :, cut], wq_up[:, i % 2, :].rearrange("p (k h) -> p k h", h=P),
                                            up_hi[:, :, cut].bitcast(F32), ALU.subtract).then_inc(wlo_done, 1)
                else:
                    nc.gpsimd.tensor_tensor(dn_lo[:, i, :], wq_dn[:, i % 2, :], dn_hi[:, i, :].bitcast(F32),
                                            ALU.subtract).then_inc(wlo_done, 1)

            def weight_scale(n):
                i = n // 2
                raw = (wq_dn if n % 2 else wq_up)[:, i % 2, :].rearrange("p (b e) -> p b e", e=BLOCK)
                scale = scales[:, i % 4, NB:NB + DB, None] if n % 2 else scales[:, i % 4, 0:NB, None]
                pool.wait_ge(scale_in[i % 4], 16 * (i // 4 + 1))
                pool.wait_ge(centred, n - BY_DVE + 1)
                nc.gpsimd.tensor_tensor(raw, raw, scale.broadcast_to([P, D // BLOCK, BLOCK]),
                                        ALU.mult).then_inc(pool_deq_done, 1)

            pool.wait_ge(par_in, 32)
            pool.wait_ge(const_set, 3)
            nc.gpsimd.tensor_tensor(expo[:, 0, :], base[:], par[:, 0, :], ALU.pow).then_inc(par_step, 1)
            ln1(0)
            nc.gpsimd.tensor_scalar(expo[:, 1, :], par[:, 1, :], 0.0, -1.0, ALU.max, ALU.mult).then_inc(par_step, 1)
            nc.gpsimd.tensor_scalar(expo[:, 2, :], par[:, 1, :], 0.0, None, ALU.min).then_inc(par_step, 1)
            pool.wait_ge(par_step, 3)
            nc.gpsimd.tensor_scalar(expo[:, 0, :], expo[:, 0, :], -1.0, None, ALU.mult).then_inc(par_step, 1)
            nc.gpsimd.tensor_tensor(alpha[:], base[:], expo[:, 1, :], ALU.pow).then_inc(par_done, 1)
            pool.wait_ge(par_step, 4)
            nc.gpsimd.tensor_tensor(omega[:], base[:], expo[:, 0, :], ALU.pow).then_inc(par_done, 1)
            nc.gpsimd.tensor_tensor(beta[:], base[:], expo[:, 2, :], ALU.pow).then_inc(par_done, 1)

            for n in (0, 1, 2):
                weight_lo(n)
            wkv(0, 0)
            weight_scale(4)
            weight_lo(3)
            weight_scale(5)
            weight_scale(6)
            wkv(0, 1)
            weight_lo(4)
            weight_scale(7)
            weight_lo(5)
            wkv(0, 2)
            weight_lo(6)
            weight_scale(8)
            weight_scale(9)
            wkv(0, 3)
            weight_lo(7)
            weight_scale(10)
            weight_lo(8)
            weight_scale(11)
            weight_lo(9)
            ln2(0)
            for n in range(12, EARLY):
                weight_lo(n - 2)
                weight_scale(n)
            for n in range(EARLY - 2, EARLY):
                weight_lo(n)
            pool.wait_ge(bias_dn_in, 16)
            pool.wait_ge(rows_done, 2)
            pool.wait_ge(wt_done, EARLY)

            def pair(p, is_first, is_last):
                for i in range(HT):
                    before, behind = weight_tiles(i) if is_first else ([], [])
                    for n in before:
                        weight_lo(n)
                    if i >= 1:
                        hidden_lo(p, i, is_first)
                    for n in behind:
                        weight_lo(n)
                    if i in (2, 3):
                        residual(p, 2 * (i - 2), is_first)
                        residual(p, 2 * (i - 2) + 1, is_first)
                    if is_last:
                        continue
                    q = p + 1
                    if i == 0:
                        ln1(q)
                    if i in (4, 5, 7, 8):
                        wkv(q, (4, 5, 7, 8).index(i))
                    if i == 12:
                        ln2(q)

            pair(0, True, False)
            with pool.Fori(1, NPAIR - 1) as p:
                pair(p, False, False)
            pair(NPAIR - 1, False, True)

        @block.scalar
        def _(act):
            def weight_centre(n):
                i = n // 2
                raw = (wq_dn if n % 2 else wq_up)[:, i % 2, :]
                act.wait_ge((qdn_in if n % 2 else qup_in)[i % 2], 16 * (i // 2 + 1))
                nc.scalar.activation(raw, raw.bitcast(I32), ACT.Copy, bias=-ZERO).then_inc(centred, 1)

            def weight_hi(n):
                i = n // 2
                full = (wq_dn if n % 2 else wq_up)[:, i % 2, :]
                act.wait_ge(wt_done, n + 1)
                nc.scalar.activation(full, weight_bank(n)[:], ACT.Copy).then_inc(full_done, 1)
                act.wait_ge(full_done, n + 1)
                if n % 2 == 0:
                    nc.scalar.activation(up_hi[:, :, i * P:(i + 1) * P], full.rearrange("p (k h) -> p k h", h=P),
                                         ACT.Copy).then_inc(whi_done, 1)
                else:
                    nc.scalar.activation(dn_hi[:, i, :], full, ACT.Copy).then_inc(whi_done, 1)

            def exp_k(q, j):
                nc.scalar.activation(mix[:, j, :], mix[:, j, :], ACT.Exp, bias=shift1[:, j:j + 1],
                                     scale=rstd1[:, j:j + 1]).then_inc(e_done, 1)

            def exp_scaled(q, c, is_first, bank):
                act.wait_ge(et_done, KT * q + c + 1)
                if not is_first or c >= 1:
                    act.wait_ge(pastb_done, 3 * (KT * q + c))
                nc.scalar.activation(ea[:], bank[:], ACT.Copy, scale=alpha[:, c:c + 1]).then_inc(ea_done, 1)

            def kv_scaled(q, c, is_first):
                act.wait_ge(kv_done, KT * q + c + 1)
                if not is_first or c >= 1:
                    act.wait_ge(pasta_done, 3 * (KT * q + c))
                nc.scalar.activation(kva[:], kv[:], ACT.Copy, scale=alpha[:, c:c + 1]).then_inc(kva_done, 1)

            def norm_hi(q, k, bank):
                act.wait_ge(nt_done, KT * q + k + 1)
                nc.scalar.activation(n_hi[:, k, :], bank[:], ACT.Copy).then_inc(nhi_done, 1)

            def hidden(p, i, is_first):
                act.wait_ge(up_done, HT * p + i + 1)
                if not is_first or i >= 1:
                    act.wait_ge(hlo_done, HT * p + i)
                nc.scalar.activation(relu[:], y1[i % 2][:], ACT.Relu, bias=bias_up[:, i:i + 1]).then_inc(relu_done, 1)
                if not is_first or i >= 2:
                    act.wait_ge(down_done, HT * p + i - 1)
                act.wait_ge(relu_done, HT * p + i + 1)
                nc.scalar.activation(h_hi[:, i % 2, :], relu[:], ACT.Copy).then_inc(hhi_done, 1)

            act.wait_ge(ln1_done, 1)
            for j in range(JT):
                exp_k(0, j)
            act.wait_ge(par_done, 1)
            exp_scaled(0, 0, True, turn[0])
            kv_scaled(0, 0, True)
            exp_scaled(0, 1, True, turn[1])
            for n in (0, 1, 2):
                weight_hi(n)
            kv_scaled(0, 1, True)
            exp_scaled(0, 2, True, turn[0])
            weight_centre(4)
            weight_hi(3)
            weight_centre(5)
            weight_centre(6)
            kv_scaled(0, 2, True)
            exp_scaled(0, 3, True, turn[1])
            weight_hi(4)
            weight_centre(7)
            weight_hi(5)
            weight_hi(6)
            kv_scaled(0, 3, True)
            weight_centre(8)
            weight_centre(9)
            weight_hi(7)
            weight_centre(10)
            weight_hi(8)
            weight_centre(11)
            weight_hi(9)
            for n in range(12, EARLY):
                weight_hi(n - 2)
                weight_centre(n)
            for k in range(KT):
                norm_hi(0, k, n_bank0[k])
            for n in range(EARLY - 2, EARLY):
                weight_hi(n)
            act.wait_ge(bias_up_in, 16)

            def pair(p, is_first, is_last):
                for i in range(HT):
                    before, behind = weight_tiles(i) if is_first else ([], [])
                    for n in before:
                        weight_hi(n)
                    hidden(p, i, is_first)
                    for n in behind:
                        weight_hi(n)
                    if is_last:
                        continue
                    q = p + 1
                    if i in (1, 2):
                        act.wait_ge(ln1_done, q + 1)
                        exp_k(q, 2 * (i - 1))
                        exp_k(q, 2 * (i - 1) + 1)
                    if 4 <= i < 4 + KT:
                        kv_scaled(q, i - 4, False)
                    if 3 <= i < 3 + KT:
                        exp_scaled(q, i - 3, False, turn[1] if is_first else turn[(i - 3) % 2])
                if not is_last:
                    for k in range(KT):
                        norm_hi(q, k, n_bank[k])

            pair(0, True, False)
            with act.Fori(1, NPAIR - 1) as p:
                pair(p, False, False)
            pair(NPAIR - 1, False, True)

        @block.vector
        def _(dve):
            def dequantise(n):
                i = n // 2
                raw = (wq_dn if n % 2 else wq_up)[:, i % 2, :].rearrange("p (b e) -> p b e", e=BLOCK)
                scale = scales[:, i % 4, NB:NB + DB, None] if n % 2 else scales[:, i % 4, 0:NB, None]
                dve.wait_ge(scale_in[i % 4], 16 * (i // 4 + 1))
                dve.wait_ge((qdn_in if n % 2 else qup_in)[i % 2], 16 * (i // 2 + 1))
                nc.vector.scalar_tensor_tensor(out=raw, in0=raw.bitcast(I32), scalar=-ZERO,
                                               in1=scale.broadcast_to([P, D // BLOCK, BLOCK]),
                                               op0=ALU.add, op1=ALU.mult).then_inc(deq_done, 1)

            def split_rows():
                dve.wait_ge(lora_in, 16)
                nc.vector.tensor_copy(rows[:], rows_raw).then_inc(rows_hi, 1)
                dve.wait_ge(rows_hi, 1)
                for a in (0, LORA_DN):
                    nc.vector.tensor_tensor(rows[a:a + 2 * RANK, :], rows_raw[a:a + 2 * RANK, :],
                                            rows[a:a + 2 * RANK, :].bitcast(F32), ALU.subtract).then_inc(rows_lo, 1)
                dve.wait_ge(rows_lo, 2)
                for a in (0, LORA_DN):
                    nc.vector.tensor_copy(rows[a:a + RANK, :], rows_raw[a:a + RANK, :]).then_inc(rows_done, 1)

            def split_cols(i):
                m = i - EARLY // 2
                dve.wait_ge(col_in[i % 2], 16 * (i // 2 + 1))
                if m >= 2:
                    dve.wait_ge(wt_done, 2 * (i - 1))
                nc.vector.tensor_copy(cols[:, i % 2, :], cols_raw[:, i % 2, :]).then_inc(cols_hi, 1)
                dve.wait_ge(cols_hi, m + 1)
                for a in (2 * RANK, LORA_DN + 2 * RANK):
                    nc.vector.tensor_tensor(cols[a:a + RANK, i % 2, :], cols_raw[a:a + RANK, i % 2, :],
                                            cols[a:a + RANK, i % 2, :].bitcast(F32),
                                            ALU.subtract).then_inc(cols_done, 1)

            def prepare(first, last):
                for n in range(first, last + 1):
                    dequantise(n)
                    if n % 2 == 0:
                        split_cols(n // 2)

            def stats1(q):
                for j in range(JT):
                    dve.wait_ge(x_mix[j], 16 * q + 16)
                    nc.vector.bn_stats(st1[:, j, :], mix[:, j, :]).then_inc(bn1_done, 1)
                dve.wait_ge(bn1_done, JT * q + JT)
                dve.sem_inc(stats_there, 1)
                for j in range(JT):
                    nc.vector.bn_aggr(mv1[:, j, :], st1[:, j, :]).then_inc(mv1_done, 1)

            def scan(state, step, c, done):
                for s in range(2):
                    a = s * SEQ
                    nc.vector.tensor_tensor_scan(state[:, a + 1:a + SEQ],
                                                 omega[:, c:c + 1].broadcast_to([P, SEQ - 1]),
                                                 step[:, a:a + SEQ - 1], 0.0, ALU.mult, ALU.add).then_inc(done, 1)
                nc.vector.tensor_copy(state[:, 0:PAIR:SEQ], step[:, 0:PAIR:SEQ]).then_inc(done, 1)

            def denominator(q, c, is_first, e_t):
                done = KT * q + c
                dve.wait_ge(ea_done, done + 1)
                dve.wait_ge(v_in[c % 2], 32 * q + 16 * (c // 2 + 1))
                if not is_first or c >= 1:
                    dve.wait_ge(num_done, done)
                nc.vector.tensor_tensor(kv[:], e_t[:], vin[:, c % 2, :], ALU.mult).then_inc(kv_done, 1)
                scan(past, ea, c, pastb_done)
                if not is_first or c >= 1:
                    dve.wait_ge(wkv_done, done)
                dve.wait_ge(pastb_done, 3 * done + 3)
                nc.vector.scalar_tensor_tensor(out=den[:], in0=e_t[:], scalar=beta[:, c:c + 1], in1=past[:],
                                               op0=ALU.mult, op1=ALU.add).then_inc(den_done, 1)
                dve.wait_ge(den_done, done + 1)
                nc.vector.reciprocal(den[:], den[:]).then_inc(rec_done, 1)

            def numerator(q, c):
                done = KT * q + c
                dve.wait_ge(kva_done, done + 1)
                scan(past, kva, c, pasta_done)
                dve.wait_ge(pasta_done, 3 * done + 3)
                nc.vector.scalar_tensor_tensor(out=mix[:, :, c * P:(c + 1) * P],
                                               in0=kv[:].rearrange("p (j t) -> p j t", t=P),
                                               scalar=beta[:, c:c + 1],
                                               in1=past[:].rearrange("p (j t) -> p j t", t=P),
                                               op0=ALU.mult, op1=ALU.add).then_inc(num_done, 1)

            def add_x(q, j, bank):
                dve.wait_ge(x_in[j], 16 * q + 16)
                dve.wait_ge(yt_done, JT * q + j + 1)
                nc.vector.tensor_tensor(xin[:, j, :], bank[:], xin[:, j, :], ALU.add).then_inc(x1_done, 1)

            def stats2(q, j):
                dve.wait_ge(x1_done, JT * q + j + 1)
                nc.vector.bn_stats(st2[:, j, :], xin[:, j, :]).then_inc(bn2_done, 1)

            def norm(q, banks, prepare_too):
                for j in (0, 2):
                    add_x(q, j, banks[j])
                    add_x(q, j + 1, banks[j + 1])
                    if prepare_too:
                        prepare(EARLY + 14 + j // 2, EARLY + 14 + j // 2)
                    stats2(q, j)
                    stats2(q, j + 1)
                dve.wait_ge(bn2_done, JT * q + JT)
                dve.sem_inc(stats_there, 1)
                for j in range(JT):
                    nc.vector.bn_aggr(mv2[:, j, :], st2[:, j, :]).then_inc(mv2_done, 1)
                if prepare_too:
                    prepare(EARLY + 16, 2 * HT - 1)
                dve.wait_ge(ln2_done, q + 1)
                for j in range(JT):
                    nc.vector.tensor_scalar(mix[:, j, :], xin[:, j, :], mv2[:, j, 0:1], rstd2[:, j:j + 1],
                                            ALU.subtract, ALU.mult).then_inc(n_done, 1)

            def norm_lo(q, k, bank):
                dve.wait_ge(nhi_done, KT * q + k + 1)
                nc.vector.tensor_tensor(n_lo[:, k, :], bank[:], n_hi[:, k, :].bitcast(F32),
                                        ALU.subtract).then_inc(nlo_done, 1)

            def hidden_lo0(p):
                dve.wait_ge(hhi_done, HT * p + 1)
                nc.vector.tensor_tensor(h_lo[:, 0, :], relu[:], h_hi[:, 0, :].bitcast(F32),
                                        ALU.subtract).then_inc(hlo_done, 1)

            def output(p, t):
                dve.wait_ge(res_done, JT * p + t + 1)
                if t < JT - 1:
                    dve.wait_ge(acc_done, (JT - 1) * p + t + 1)
                else:
                    dve.wait_ge(down_done, HT * p + HT)
                nc.vector.tensor_tensor(res[:, t, :], acc[t][:], res[:, t, :], ALU.add).then_inc(out_done, 1)

            stats1(0)
            for n in range(BY_DVE):
                dequantise(n)
            dve.wait_ge(par_done, 3)
            for c in range(KT):
                denominator(0, c, True, turn[c % 2])
                numerator(0, c)
            norm(0, acc, False)
            for k in range(KT):
                norm_lo(0, k, n_bank0[k])
            split_rows()

            def pair(p, is_first, is_last):
                if not is_last:
                    q = p + 1
                    banks = [turn[1]] * 4 if is_first else turn * 2
                    if is_first:
                        prepare(EARLY, EARLY + 1)
                    else:
                        stats1(q)
                    hidden_lo0(p)
                    if is_first:
                        prepare(EARLY + 2, EARLY + 3)
                        stats1(q)
                        prepare(EARLY + 4, EARLY + 5)
                    for c in range(KT):
                        denominator(q, c, False, banks[c])
                        if is_first:
                            n = EARLY + (6, 7, 9, 11)[c]
                            prepare(n, n)
                        numerator(q, c)
                        if is_first and c >= 1:
                            n = EARLY + (8, 10, 12)[c - 1]
                            prepare(n, n)
                    if is_first:
                        prepare(EARLY + 13, EARLY + 13)
                    norm(q, banks, is_first)
                    for k in range(KT):
                        norm_lo(q, k, n_bank[k])
                else:
                    hidden_lo0(p)
                for t in range(JT):
                    output(p, t)

            pair(0, True, False)
            with dve.Fori(1, NPAIR - 1) as p:
                pair(p, False, False)
            pair(NPAIR - 1, False, True)

        @block.tensor
        def _(pe):
            def weights(n):
                i, bank = n // 2, weight_bank(n)
                raw = (wq_dn if n % 2 else wq_up)[:, i % 2, :]
                if n < BY_DVE:
                    pe.wait_ge(deq_done, n + 1)
                elif n < EARLY:
                    pe.wait_ge(pool_deq_done, n - BY_DVE + 1)
                else:
                    pe.wait_ge(deq_done, n - EARLY + BY_DVE + 1)
                if n > EARLY:
                    pe.wait_ge(full_done, n)
                elif n == EARLY:
                    pe.wait_ge(nlo_done, 1)
                elif n >= 2:
                    pe.wait_ge(full_done, n - 1)
                for k in range(KT):
                    nc.tensor.matmul(bank[:, k * P:(k + 1) * P], raw[:, k * P:(k + 1) * P], ident[:],
                                     start=(k == 0), stop=False, is_transpose=True, skip_group_check=True)
                if n < EARLY:
                    pe.wait_ge(col_in[i % 2], 16 * (i // 2 + 1))
                    a, c, size = rows_raw, cols_raw[:, i % 2, :], RANK
                else:
                    pe.wait_ge(cols_done, 2 * (i - EARLY // 2) + 2)
                    a, c, size = rows, cols[:, i % 2, :], LORA
                if n % 2 == 0:
                    for k in range(KT):
                        last = nc.tensor.matmul(bank[:, k * P:(k + 1) * P], a[0:size, k * P:(k + 1) * P],
                                                c[0:size, :], start=False, stop=(k == KT - 1),
                                                skip_group_check=True)
                else:
                    last = nc.tensor.matmul(bank[:], c[LORA_DN:LORA_DN + size, :], a[LORA_DN:LORA_DN + size, :],
                                            start=False, stop=True, skip_group_check=True)
                last.then_inc(wt_done, 1)

            def turn_e(q, c, bank):
                for j in range(JT):
                    last = nc.tensor.transpose(bank[:, j * P:(j + 1) * P], mix[:, j, c * P:(c + 1) * P], ident[:])
                last.then_inc(et_done, 1)

            def turn_y(q, j, bank):
                for c in range(KT):
                    last = nc.tensor.transpose(bank[:, c * P:(c + 1) * P], mix[:, j, c * P:(c + 1) * P], ident[:])
                last.then_inc(yt_done, 1)

            def turn_n(q, k, bank):
                if k == 0:
                    pe.wait_ge(n_done, JT * q + JT)
                for j in range(JT):
                    last = nc.tensor.transpose(bank[:, j * P:(j + 1) * P], mix[:, j, k * P:(k + 1) * P], ident[:])
                last.then_inc(nt_done, 1)

            def up(p, i, is_first):
                if not is_first or i >= 2:
                    pe.wait_ge(relu_done, HT * p + i - 1)
                if is_first:
                    pe.wait_ge(wlo_done, 2 * i + 1)
                cut = slice(i * P, (i + 1) * P)
                for k in range(KT):
                    if i == 0:
                        pe.wait_ge(nlo_done, KT * p + k + 1)
                    nc.tensor.matmul(y1[i % 2][:], up_hi[:, k, cut], n_hi[:, k, :], start=(k == 0), stop=False)
                    nc.tensor.matmul(y1[i % 2][:], up_hi[:, k, cut], n_lo[:, k, :], start=False, stop=False)
                    last = nc.tensor.matmul(y1[i % 2][:], up_lo[:, k, cut], n_hi[:, k, :], start=False,
                                            stop=(k == KT - 1))
                last.then_inc(up_done, 1)

            def down(p, i, is_first):
                pe.wait_ge(hlo_done, HT * p + i + 1)
                if is_first:
                    pe.wait_ge(wlo_done, 2 * i + 2)
                for t in range(JT):
                    if i == 0 and not is_first:
                        pe.wait_ge(out_done, JT * p - JT + t + 1)
                    rows = slice(t * P, (t + 1) * P)
                    hi, lo = h_hi[:, i % 2, rows], h_lo[:, i % 2, rows]
                    nc.tensor.matmul(acc[t][:], hi, dn_hi[:, i, :], start=(i == 0), stop=False)
                    nc.tensor.matmul(acc[t][:], hi, dn_lo[:, i, :], start=False, stop=False)
                    last = nc.tensor.matmul(acc[t][:], lo, dn_hi[:, i, :], start=False, stop=(i == HT - 1))
                    if i == HT - 1 and t < JT - 1:
                        last.then_inc(acc_done, 1)
                last.then_inc(down_done, 1)

            pe.wait_ge(id_done, 1)
            def turn_y0(c):
                pe.wait_ge(wkv_done, c + 1)
                for j in range(JT):
                    last = nc.tensor.transpose(acc[j][:, c * P:(c + 1) * P], mix[:, j, c * P:(c + 1) * P], ident[:])
                    if c == KT - 1:
                        last.then_inc(yt_done, 1)

            pe.wait_ge(lora_in, 16)
            pe.wait_ge(e_done, JT)
            turn_e(0, 0, turn[0])
            weights(0)
            turn_e(0, 1, turn[1])
            weights(1)
            pe.wait_ge(den_done, 1)
            turn_e(0, 2, turn[0])
            weights(2)
            weights(3)
            turn_y0(0)
            pe.wait_ge(den_done, 2)
            turn_e(0, 3, turn[1])
            for c in (1, 2):
                weights(2 * c + 2)
                weights(2 * c + 3)
                turn_y0(c)
            for n in (8, 9):
                weights(n)
            turn_y0(3)
            for n in (10, 11):
                weights(n)
            for k in range(KT):
                turn_n(0, k, n_bank0[k])
            for n in range(12, EARLY):
                weights(n)
            pe.wait_ge(full_done, EARLY)

            def pair(p, is_first, is_last):
                q = p + 1
                for i in range(HT):
                    if i == HT - 1 and not is_last:
                        if is_first:
                            pe.wait_ge(full_done, 2 * HT)
                        pe.wait_ge(relu_done, HT * p + HT - 1)
                        for k in range(KT - 1):
                            turn_n(q, k, n_bank[k])
                    before, behind = weight_tiles(i) if is_first else ([], [])
                    for n in before:
                        weights(n)
                    up(p, i, is_first)
                    for n in behind:
                        weights(n)
                    if not is_last and 3 <= i < 3 + KT:
                        c = i - 3
                        if c == 0:
                            pe.wait_ge(e_done, JT * q + JT)
                        if is_first and c == 0:
                            pe.wait_ge(nlo_done, KT * q)
                        elif is_first:
                            pe.wait_ge(den_done, KT * q + c)
                        elif c < 2:
                            pe.wait_ge(nlo_done, KT * q - 2 + c)
                        else:
                            pe.wait_ge(den_done, KT * q + c - 1)
                        turn_e(q, c, turn[1] if is_first else turn[c % 2])
                    if not is_last and i in (10, 11):
                        for j in (2 * (i - 10), 2 * (i - 10) + 1):
                            if j == 0:
                                pe.wait_ge(wkv_done, KT * q + KT)
                            if is_first and j == 0:
                                pe.wait_ge(den_done, KT * q + KT)
                            elif is_first:
                                pe.wait_ge(x1_done, JT * q + j)
                            elif j < 2:
                                pe.wait_ge(den_done, KT * q + 3 + j)
                            else:
                                pe.wait_ge(x1_done, JT * q + j - 1)
                            turn_y(q, j, turn[1] if is_first else turn[j % 2])
                    if i >= 1:
                        down(p, i - 1, is_first)
                if not is_last:
                    pe.wait_ge(relu_done, HT * q)
                    turn_n(q, KT - 1, n_bank[KT - 1])
                down(p, HT - 1, is_first)

            pair(0, True, False)
            with pe.Fori(1, NPAIR - 1) as p:
                pair(p, False, False)
            pair(NPAIR - 1, False, True)


def kernel(x, ctx_2048, L0_xattn_time_decay, L0_xattn_time_first, L0_ffn_w_up_q, L0_ffn_w_up_scale,
           L0_ffn_b_up, L0_ffn_w_up_lora_a, L0_ffn_w_up_lora_b, L0_ffn_w_down_q, L0_ffn_w_down_scale,
           L0_ffn_b_down, L0_ffn_w_down_lora_a, L0_ffn_w_down_lora_b):
    import numpy as np
    import concourse.bacc as bacc
    from concourse.bass_utils import run_bass_kernel_spmd

    def lay(a):
        return np.ascontiguousarray(a)

    gap = np.zeros((LORA_DN - LORA, 1), np.float32)
    a_up, b_up_l = np.asarray(L0_ffn_w_up_lora_a), np.asarray(L0_ffn_w_up_lora_b)
    a_dn, b_dn_l = np.asarray(L0_ffn_w_down_lora_a), np.asarray(L0_ffn_w_down_lora_b)
    rows = np.concatenate([a_up.T] * 3 + [gap.repeat(D, 1)] + [b_dn_l] * 3)
    cols = np.concatenate([b_up_l] * 3 + [gap.repeat(HID, 1)] + [a_dn.T] * 3)
    arrays = {
        "x": lay(np.asarray(x).reshape(BATCH * SEQ, D)),
        "ctx_t": lay(np.asarray(ctx_2048).transpose(2, 0, 1).reshape(D, BATCH * SEQ)),
        "decay": lay(np.asarray(L0_xattn_time_decay).reshape(KT, P).T),
        "first": lay(np.asarray(L0_xattn_time_first).reshape(KT, P).T),
        "q_up": lay(np.asarray(L0_ffn_w_up_q).reshape(HT, P, D)),
        "q_dn": lay(np.asarray(L0_ffn_w_down_q).reshape(KT, P, HT, P).transpose(2, 1, 0, 3).reshape(HT, P, D)),
        "w_scales": lay(np.concatenate([
            np.asarray(L0_ffn_w_up_scale).reshape(HT, P, NB),
            np.asarray(L0_ffn_w_down_scale).reshape(KT, P, HT, P // BLOCK).transpose(2, 1, 0, 3).reshape(HT, P, DB),
        ], axis=2)),
        "b_up": lay(np.asarray(L0_ffn_b_up).reshape(HT, P).T),
        "b_dn": lay(np.asarray(L0_ffn_b_down).reshape(1, D)),
        "lora_rows": lay(rows),
        "lora_cols": lay(cols.reshape(LORA_ROWS, HT, P).transpose(1, 0, 2)),
    }
    nc = bacc.Bacc("TRN2", target_bir_lowering=False, num_devices=1)
    args = [nc.dram_tensor(f"in_{n}", a.shape, mybir.dt.from_np(a.dtype), kind="ExternalInput").ap()
            for n, a in arrays.items()]
    out = nc.dram_tensor("out", (BATCH * SEQ, D), F32, kind="ExternalOutput").ap()
    build(nc, *args, out)
    done = run_bass_kernel_spmd(nc, [{f"in_{n}": a for n, a in arrays.items()}], core_ids=[0])
    return done.results[0]["out"].reshape(BATCH, SEQ, D)
```

```python
from contextlib import ExitStack

import concourse.bass as bass
from concourse import mybir

F32 = mybir.dt.float32
F32R = mybir.dt.float32r
I32 = mybir.dt.int32
ALU = mybir.AluOpType
ACT = mybir.ActivationFunctionType

P = 128
BATCH = 16
SEQ = 256
D = 512
HID = 2048
RANK = 16
BLOCK = 64
ZERO = 7.5
EPS = 1e-5
PAIR = 2 * SEQ
NPAIR = BATCH * SEQ // PAIR
KT = D // P
HT = HID // P
JT = PAIR // P
NB = D // BLOCK
DB = KT * (P // BLOCK)
LORA = 3 * RANK
LORA_DN = 64
LORA_ROWS = LORA_DN + LORA

BY_DVE = 1
EARLY = 4
BN = 6

FIRST, SECOND, ALL = range(0, JT // 2), range(JT // 2, JT), range(JT)


def columns(js):
    return slice(js[0] * P, (js[-1] + 1) * P)


def pair_of(u, js):
    return u - 1 if js == ALL else 0


def tokens(u, js):
    return JT * (u - 1) if js == ALL else js[0]


def outputs_before(u, js):
    return (JT - 1) * (u - 1) - 1 if js == ALL else u


def build(nc, x, ctx_t, decay, first, q_up, q_dn, w_scales, b_up, b_dn, lora_rows, lora_cols, out):
    xt = x.rearrange("(n j p) d -> n j p d", p=P, j=JT)
    ot = out.rearrange("(n j p) d -> n j p d", p=P, j=JT)
    vt = ctx_t.rearrange("(c p) (n t) -> n c p t", p=P, t=PAIR)

    with ExitStack() as ctx:
        def sb(name, shape, dt=F32):
            return ctx.enter_context(nc.sbuf_tensor(name, shape, dt))

        def psum(name):
            return ctx.enter_context(nc.psum_tensor(name, [P, 512], F32))

        def sem(name):
            return ctx.enter_context(nc.semaphore(name))

        up_hi = sb("up_hi", [P, KT, HID], F32R)
        up_lo = sb("up_lo", [P, KT, HID], F32R)
        dn_hi = sb("dn_hi", [P, HT, D], F32R)
        dn_lo = sb("dn_lo", [P, HT, D], F32R)
        wq_up = sb("wq_up", [P, 2, D])
        wq_dn = sb("wq_dn", [P, 2, D])
        scales = sb("scales", [P, 4, NB + DB])
        rows = sb("rows", [LORA_ROWS, D], F32R)
        cols_raw = sb("cols_raw", [LORA_ROWS, 2, P])
        cols_split = sb("cols_split", [LORA_ROWS, 2, P], F32R)
        bias_up = sb("bias_up", [P, HT])
        bias_dn = sb("bias_dn", [P, D])
        ident = sb("ident", [P, P])
        par = sb("par", [P, 2, KT])
        base = sb("base", [P, KT])
        half = sb("half", [P, JT])
        eps = sb("eps", [P, JT])
        expo = sb("expo", [P, 3, KT])
        omega = sb("omega", [P, KT])
        alpha = sb("alpha", [P, KT])
        beta = sb("beta", [P, KT])
        xin = sb("xin", [P, JT, D])
        mix = sb("mix", [P, JT, D])
        res = sb("res", [P, JT, D])
        rows_raw = res[0:LORA_ROWS, 0, :]
        st1 = sb("st1", [P, JT, BN])
        st2 = sb("st2", [P, JT, BN])
        mv1 = sb("mv1", [P, JT, 2])
        mv2 = sb("mv2", [P, JT, 2])
        var1 = sb("var1", [P, JT])
        var2 = sb("var2", [P, JT])
        rstd1 = sb("rstd1", [P, JT])
        rstd2 = sb("rstd2", [P, JT])
        neg1 = sb("neg1", [P, JT])
        shift1 = sb("shift1", [P, JT])
        vin = sb("vin", [P, 2, PAIR])
        ea = sb("ea", [P, PAIR])
        kv = sb("kv", [P, PAIR])
        kva = sb("kva", [P, PAIR])
        past = sb("past", [P, PAIR])
        den = sb("den", [P, PAIR])
        n_hi = sb("n_hi", [P, KT, PAIR], F32R)
        n_lo = sb("n_lo", [P, KT, PAIR], F32R)
        relu = sb("relu", [P, PAIR])
        h_hi = sb("h_hi", [P, 2, PAIR], F32R)
        h_lo = sb("h_lo", [P, 2, PAIR], F32R)

        turn = [psum("turn0"), psum("turn1")]
        y1 = [psum("y1_0"), psum("y1_1")]
        acc = [psum(f"acc{t}") for t in range(JT)]

        par_in = sem("par_in")
        lora_in = sem("lora_in")
        bias_up_in = sem("bias_up_in")
        bias_dn_in = sem("bias_dn_in")
        qup_in = [sem(f"qup_in{s}") for s in range(2)]
        qdn_in = [sem(f"qdn_in{s}") for s in range(2)]
        scale_in = [sem(f"scale_in{s}") for s in range(4)]
        col_in = [sem(f"col_in{s}") for s in range(2)]
        x_mix = [sem(f"x_mix{j}") for j in range(JT)]
        x_in = [sem(f"x_in{j}") for j in range(JT)]
        v_in = [sem(f"v_in{s}") for s in range(2)]
        stored = [sem(f"stored{j}") for j in range(JT)]
        const_set = sem("const_set")
        id_zero = sem("id_zero")
        id_done = sem("id_done")
        par_step = sem("par_step")
        par_done = sem("par_done")
        rows_hi = sem("rows_hi")
        rows_lo = sem("rows_lo")
        rows_done = sem("rows_done")
        cols_hi = sem("cols_hi")
        cols_done = sem("cols_done")
        deq_done = sem("deq_done")
        centred = sem("centred")
        scaled = sem("scaled")
        wt_done = sem("wt_done")
        whi_done = sem("whi_done")
        wlo_done = sem("wlo_done")
        bn1_done = sem("bn1_done")
        mv1_done = sem("mv1_done")
        stats_there = sem("stats_there")
        ln1_step = sem("ln1_step")
        ln1_done = sem("ln1_done")
        e_done = sem("e_done")
        et_done = sem("et_done")
        ea_done = sem("ea_done")
        kv_done = sem("kv_done")
        kva_done = sem("kva_done")
        pastb_done = sem("pastb_done")
        den_done = sem("den_done")
        rec_done = sem("rec_done")
        pasta_done = sem("pasta_done")
        num_done = sem("num_done")
        wkv_done = sem("wkv_done")
        yt_done = sem("yt_done")
        x1_done = sem("x1_done")
        bn2_done = sem("bn2_done")
        mv2_done = sem("mv2_done")
        ln2_step = sem("ln2_step")
        ln2_done = sem("ln2_done")
        n_done = sem("n_done")
        nt_done = sem("nt_done")
        nhi_done = sem("nhi_done")
        nlo_done = sem("nlo_done")
        up_done = sem("up_done")
        relu_done = sem("relu_done")
        hhi_done = sem("hhi_done")
        hlo_done = sem("hlo_done")
        down_done = sem("down_done")
        acc_done = sem("acc_done")
        res_done = sem("res_done")
        out_done = sem("out_done")

        weight_bank = [y1[0], y1[1]] + [acc[2], acc[3]] * (HT - 1)
        n_bank = [y1[0], turn[0], turn[1], y1[1]]

        block = ctx.enter_context(nc.Block())

        @block.sync
        def _(sp):
            def load_weights(n):
                i = n // 2
                if n >= 4:
                    sp.wait_ge(wt_done, n - 3)
                if n % 2 == 0:
                    sp.dma_start(scales[:, i % 4, :], w_scales[i]).then_inc(scale_in[i % 4], 16)
                    sp.dma_start(wq_up[:, i % 2, :].bitcast(I32), q_up[i]).then_inc(qup_in[i % 2], 16)
                else:
                    sp.dma_start(wq_dn[:, i % 2, :].bitcast(I32), q_dn[i]).then_inc(qdn_in[i % 2], 16)
                    sp.dma_start(cols_raw[:, i % 2, :], lora_cols[i]).then_inc(col_in[i % 2], 16)

            def load_mix(q, j):
                sp.dma_start(mix[:, j, :], xt[q, j]).then_inc(x_mix[j], 16)

            def load_x(q, j):
                sp.dma_start(xin[:, j, :], xt[q, j]).then_inc(x_in[j], 16)

            def load_v(u, js, c):
                if not (js == FIRST and c < 2):
                    sp.wait_ge(kv_done, KT * u + c - 1)
                cols = columns(js)
                sp.dma_start(vin[:, c % 2, cols], vt[pair_of(u, js), c, :, cols]).then_inc(v_in[c % 2], 16)

            def store(p, j):
                sp.wait_ge(out_done, JT * p + j + 1)
                sp.dma_start(ot[p, j], res[:, j, :]).then_inc(stored[j], 16)

            for j in FIRST:
                load_mix(0, j)
            sp.dma_start(par[:, 0, :], decay).then_inc(par_in, 16)
            sp.dma_start(par[:, 1, :], first).then_inc(par_in, 16)
            load_weights(0)
            sp.dma_start(rows_raw, lora_rows).then_inc(lora_in, 16)
            load_v(0, FIRST, 0)
            load_weights(1)
            for j in SECOND:
                load_mix(0, j)
            load_v(0, FIRST, 1)
            load_weights(2)
            load_weights(3)
            for j in range(JT):
                load_x(0, j)
            sp.dma_start(bias_up[:], b_up).then_inc(bias_up_in, 16)
            sp.dma_start(bias_dn[:], b_dn.broadcast_to([P, D])).then_inc(bias_dn_in, 16)
            load_weights(4)
            load_v(0, FIRST, 2)
            load_weights(5)
            load_v(0, FIRST, 3)
            load_weights(6)
            load_weights(7)
            load_v(1, SECOND, 0)
            load_v(1, SECOND, 1)
            load_weights(8)
            load_weights(9)
            load_v(1, SECOND, 2)
            for n in range(10, 14):
                load_weights(n)
            load_v(1, SECOND, 3)
            for n in range(14, 30):
                load_weights(n)
            sp.wait_ge(nt_done, 2 * KT)
            for j in range(JT):
                load_mix(1, j)
            for n in range(30, 2 * HT):
                load_weights(n)
            load_v(2, ALL, 0)
            load_v(2, ALL, 1)
            for j in range(JT):
                sp.wait_ge(res_done, j + 1)
                load_x(1, j)
            load_v(2, ALL, 2)
            load_v(2, ALL, 3)
            store(0, 0)
            store(0, 1)
            sp.wait_ge(nt_done, 3 * KT)
            for j in range(JT):
                load_mix(2, j)
            load_v(3, ALL, 0)
            load_v(3, ALL, 1)
            store(0, 2)
            store(0, 3)

            def pair(p, loads):
                u = p + 2
                if loads >= 1:
                    for j in range(JT):
                        sp.wait_ge(res_done, JT * p + j + 1)
                        load_x(p + 1, j)
                    load_v(u, ALL, 2)
                    load_v(u, ALL, 3)
                if loads == 2:
                    sp.wait_ge(nt_done, KT * u + KT)
                    for j in range(JT):
                        load_mix(p + 2, j)
                    load_v(u + 1, ALL, 0)
                    load_v(u + 1, ALL, 1)
                for j in range(JT):
                    store(p, j)

            with sp.Fori(1, NPAIR - 2) as p:
                pair(p, 2)
            pair(NPAIR - 2, 1)
            pair(NPAIR - 1, 0)
            for j in range(JT):
                sp.wait_ge(stored[j], 16 * NPAIR)

        @block.gpsimd
        def _(pool):
            nc.gpsimd.memset(ident[:], 0.0).then_inc(id_zero, 1)
            nc.gpsimd.memset(base[:], 2.718281828459045).then_inc(const_set, 1)
            nc.gpsimd.memset(half[:], -0.5).then_inc(const_set, 1)
            nc.gpsimd.memset(eps[:], EPS).then_inc(const_set, 1)
            pool.wait_ge(id_zero, 1)
            nc.gpsimd.affine_select(out=ident[:], in_=ident[:], compare_op=ALU.not_equal, fill=1.0, base=0,
                                    pattern=[[-1, P]], channel_multiplier=1).then_inc(id_done, 1)

            def ln1(u, js):
                a, b = js[0], js[-1] + 1
                pool.wait_ge(mv1_done, tokens(u, js) + len(js))
                nc.gpsimd.tensor_tensor(var1[:, a:b], mv1[:, a:b, 1], eps[:, a:b], ALU.add).then_inc(ln1_step, 1)
                nc.gpsimd.tensor_scalar(neg1[:, a:b], mv1[:, a:b, 0], -1.0, None, ALU.mult).then_inc(ln1_step, 1)
                pool.wait_ge(ln1_step, 3 * u + 2)
                nc.gpsimd.tensor_tensor(rstd1[:, a:b], var1[:, a:b], half[:, a:b], ALU.pow).then_inc(ln1_step, 1)
                pool.wait_ge(ln1_step, 3 * u + 3)
                nc.gpsimd.tensor_tensor(shift1[:, a:b], neg1[:, a:b], rstd1[:, a:b], ALU.mult).then_inc(ln1_done, 1)

            def ln2(u, js):
                a, b = js[0], js[-1] + 1
                pool.wait_ge(mv2_done, tokens(u, js) + len(js))
                nc.gpsimd.tensor_tensor(var2[:, a:b], mv2[:, a:b, 1], eps[:, a:b], ALU.add).then_inc(ln2_step, 1)
                pool.wait_ge(ln2_step, u + 1)
                nc.gpsimd.tensor_tensor(rstd2[:, a:b], var2[:, a:b], half[:, a:b], ALU.pow).then_inc(ln2_done, 1)

            def wkv(u, js, c):
                pool.wait_ge(num_done, KT * u + c + 1)
                y = mix[:, js[0]:js[-1] + 1, c * P:(c + 1) * P]
                nc.gpsimd.tensor_tensor(y, y, den[:, columns(js)].rearrange("p (j t) -> p j t", t=P),
                                        ALU.mult).then_inc(wkv_done, 1)

            def residual(u, js, j):
                if js == ALL:
                    pool.wait_ge(stored[j], 16 * (u - 1))
                else:
                    pool.wait_ge(x1_done, j + 1)
                nc.gpsimd.tensor_tensor(res[:, j, :], xin[:, j, :], bias_dn[:], ALU.add).then_inc(res_done, 1)

            def hidden_lo(u, js, i):
                cols = columns(js)
                pool.wait_ge(hhi_done, HT * u + i + 1)
                if js != FIRST or i >= 2:
                    pool.wait_ge(down_done, HT * u + i - 1)
                nc.gpsimd.tensor_tensor(h_lo[:, i % 2, cols], relu[:, cols], h_hi[:, i % 2, cols].bitcast(F32),
                                        ALU.subtract).then_inc(hlo_done, 1)

            def weight_scale(n):
                i = n // 2
                raw = (wq_dn if n % 2 else wq_up)[:, i % 2, :].rearrange("p (b e) -> p b e", e=BLOCK)
                scale = scales[:, i % 4, NB:NB + DB, None] if n % 2 else scales[:, i % 4, 0:NB, None]
                pool.wait_ge(scale_in[i % 4], 16 * (i // 4 + 1))
                pool.wait_ge(centred, n - BY_DVE + 1)
                nc.gpsimd.tensor_tensor(raw, raw, scale.broadcast_to([P, D // BLOCK, BLOCK]),
                                        ALU.mult).then_inc(scaled, 1)

            pool.wait_ge(par_in, 32)
            pool.wait_ge(const_set, 3)
            nc.gpsimd.tensor_tensor(expo[:, 0, :], base[:], par[:, 0, :], ALU.pow).then_inc(par_step, 1)
            ln1(0, FIRST)
            nc.gpsimd.tensor_scalar(expo[:, 1, :], par[:, 1, :], 0.0, -1.0, ALU.max, ALU.mult).then_inc(par_step, 1)
            nc.gpsimd.tensor_scalar(expo[:, 2, :], par[:, 1, :], 0.0, None, ALU.min).then_inc(par_step, 1)
            pool.wait_ge(par_step, 3)
            nc.gpsimd.tensor_scalar(expo[:, 0, :], expo[:, 0, :], -1.0, None, ALU.mult).then_inc(par_step, 1)
            nc.gpsimd.tensor_tensor(alpha[:], base[:], expo[:, 1, :], ALU.pow).then_inc(par_done, 1)
            pool.wait_ge(par_step, 4)
            nc.gpsimd.tensor_tensor(omega[:], base[:], expo[:, 0, :], ALU.pow).then_inc(par_done, 1)
            nc.gpsimd.tensor_tensor(beta[:], base[:], expo[:, 2, :], ALU.pow).then_inc(par_done, 1)

            weight_scale(1)
            wkv(0, FIRST, 0)
            weight_scale(2)
            wkv(0, FIRST, 1)
            weight_scale(3)
            wkv(0, FIRST, 2)
            wkv(0, FIRST, 3)
            weight_scale(4)
            ln1(1, SECOND)
            ln2(0, FIRST)
            weight_scale(5)
            pool.wait_ge(bias_dn_in, 16)
            pool.wait_ge(rows_done, 2)
            pool.wait_ge(wt_done, EARLY)

            for i in range(HT):
                n = EARLY + 2 * i + 2
                if i in (2, 5):
                    wkv(1, SECOND, (2, 5).index(i) * 2)
                if n < 2 * HT:
                    weight_scale(n)
                hidden_lo(0, FIRST, i)
                if n < 2 * HT:
                    weight_scale(n + 1)
                if i in (3, 6):
                    wkv(1, SECOND, (3, 6).index(i) * 2 + 1)
                if i in (4, 7):
                    residual(0, FIRST, (4, 7).index(i))
                if i == 8:
                    ln2(1, SECOND)
                if i in (10, 11):
                    residual(1, SECOND, i - 8)
                if i == 12:
                    ln1(2, ALL)
            for i in range(HT):
                hidden_lo(1, SECOND, i)
                if i in (3, 5, 8, 10):
                    wkv(2, ALL, (3, 5, 8, 10).index(i))
                if i == 13:
                    ln2(2, ALL)

            def pair(p, is_last):
                u = p + 1
                for i in range(HT):
                    if i >= 1:
                        hidden_lo(u, ALL, i)
                    if i in (2, 3):
                        residual(u, ALL, 2 * (i - 2))
                        residual(u, ALL, 2 * (i - 2) + 1)
                    if is_last:
                        continue
                    if i == 0:
                        ln1(u + 1, ALL)
                    if i in (4, 5, 7, 8):
                        wkv(u + 1, ALL, (4, 5, 7, 8).index(i))
                    if i == 12:
                        ln2(u + 1, ALL)

            with pool.Fori(1, NPAIR - 1) as p:
                pair(p, False)
            pair(NPAIR - 1, True)

        @block.scalar
        def _(act):
            def weight_centre(n):
                i = n // 2
                raw = (wq_dn if n % 2 else wq_up)[:, i % 2, :]
                act.wait_ge((qdn_in if n % 2 else qup_in)[i % 2], 16 * (i // 2 + 1))
                nc.scalar.activation(raw, raw.bitcast(I32), ACT.Copy, bias=-ZERO).then_inc(centred, 1)

            def weight_hi(n):
                i = n // 2
                act.wait_ge(wt_done, n + 1)
                if n % 2 == 0:
                    nc.scalar.activation(up_hi[:, :, i * P:(i + 1) * P],
                                         weight_bank[n][:].rearrange("p (k h) -> p k h", h=P),
                                         ACT.Copy).then_inc(whi_done, 1)
                else:
                    nc.scalar.activation(dn_hi[:, i, :], weight_bank[n][:], ACT.Copy).then_inc(whi_done, 1)

            def exp_k(j):
                nc.scalar.activation(mix[:, j, :], mix[:, j, :], ACT.Exp, bias=shift1[:, j:j + 1],
                                     scale=rstd1[:, j:j + 1]).then_inc(e_done, 1)

            def exp_scaled(u, js, c):
                cols = columns(js)
                act.wait_ge(et_done, KT * u + c + 1)
                if js != FIRST or c >= 1:
                    act.wait_ge(pastb_done, 3 * (KT * u + c))
                nc.scalar.activation(ea[:, cols], turn[c % 2][:, cols], ACT.Copy,
                                     scale=alpha[:, c:c + 1]).then_inc(ea_done, 1)

            def kv_scaled(u, js, c):
                cols = columns(js)
                act.wait_ge(kv_done, KT * u + c + 1)
                if js != FIRST or c >= 1:
                    act.wait_ge(pasta_done, 3 * (KT * u + c))
                nc.scalar.activation(kva[:, cols], kv[:, cols], ACT.Copy,
                                     scale=alpha[:, c:c + 1]).then_inc(kva_done, 1)

            def norm_hi(u, js, k, bank):
                cols = columns(js)
                act.wait_ge(nt_done, KT * u + k + 1)
                nc.scalar.activation(n_hi[:, k, cols], bank[:, cols], ACT.Copy).then_inc(nhi_done, 1)

            def hidden(u, js, i):
                cols = columns(js)
                act.wait_ge(up_done, HT * u + i + 1)
                if js != FIRST or i >= 1:
                    act.wait_ge(hlo_done, HT * u + i)
                nc.scalar.activation(relu[:, cols], y1[i % 2][:, cols], ACT.Relu,
                                     bias=bias_up[:, i:i + 1]).then_inc(relu_done, 1)
                if js != FIRST or i >= 2:
                    act.wait_ge(down_done, HT * u + i - 1)
                act.wait_ge(relu_done, HT * u + i + 1)
                nc.scalar.activation(h_hi[:, i % 2, cols], relu[:, cols], ACT.Copy).then_inc(hhi_done, 1)

            act.wait_ge(ln1_done, 1)
            exp_k(0)
            exp_k(1)
            act.wait_ge(par_done, 1)
            exp_scaled(0, FIRST, 0)
            kv_scaled(0, FIRST, 0)
            exp_scaled(0, FIRST, 1)
            weight_centre(1)
            kv_scaled(0, FIRST, 1)
            exp_scaled(0, FIRST, 2)
            weight_centre(2)
            weight_hi(0)
            weight_centre(3)
            kv_scaled(0, FIRST, 2)
            exp_scaled(0, FIRST, 3)
            weight_hi(1)
            weight_centre(4)
            kv_scaled(0, FIRST, 3)
            weight_hi(2)
            weight_hi(3)
            weight_centre(5)
            for k in range(KT):
                norm_hi(0, FIRST, k, n_bank[k])
            act.wait_ge(ln1_done, 2)
            exp_k(2)
            exp_k(3)
            act.wait_ge(bias_up_in, 16)

            for i in range(HT):
                n = EARLY + 2 * i
                hidden(0, FIRST, i)
                if i in (3,):
                    exp_scaled(1, SECOND, 2)
                if n < 2 * HT:
                    weight_hi(n)
                if i in (1, 4):
                    kv_scaled(1, SECOND, (1, 4).index(i) * 2)
                if n + 2 < 2 * HT:
                    weight_centre(n + 2)
                if n < 2 * HT:
                    weight_hi(n + 1)
                if n + 2 < 2 * HT:
                    weight_centre(n + 3)
                if i in (2, 5):
                    kv_scaled(1, SECOND, (2, 5).index(i) * 2 + 1)
                if i in (0, 1, 4):
                    exp_scaled(1, SECOND, (0, 1, 4).index(i) + i // 4)
                if i in (9, 10):
                    for k in (2 * (i - 9), 2 * (i - 9) + 1):
                        norm_hi(1, SECOND, k, turn[k % 2])
                if i == 13:
                    act.wait_ge(ln1_done, 3)
                    exp_k(0)
                    exp_k(1)
                if i == 14:
                    exp_k(2)
                    exp_k(3)
            exp_scaled(2, ALL, 0)
            for i in range(HT):
                hidden(1, SECOND, i)
                if i in (0, 3, 6, 8):
                    kv_scaled(2, ALL, (0, 3, 6, 8).index(i))
                if i in (1, 4, 6):
                    exp_scaled(2, ALL, (1, 4, 6).index(i) + 1)
            for k in range(KT):
                norm_hi(2, ALL, k, n_bank[k])

            def pair(p, is_last):
                u = p + 1
                for i in range(HT):
                    hidden(u, ALL, i)
                    if is_last:
                        continue
                    if i == 1:
                        act.wait_ge(ln1_done, u + 2)
                    if i in (1, 2):
                        exp_k(2 * (i - 1))
                        exp_k(2 * (i - 1) + 1)
                    if 4 <= i < 4 + KT:
                        kv_scaled(u + 1, ALL, i - 4)
                    if 3 <= i < 3 + KT:
                        exp_scaled(u + 1, ALL, i - 3)
                if not is_last:
                    for k in range(KT):
                        norm_hi(u + 1, ALL, k, n_bank[k])

            with act.Fori(1, NPAIR - 1) as p:
                pair(p, False)
            pair(NPAIR - 1, True)

        @block.vector
        def _(dve):
            def dequantise(n):
                i = n // 2
                raw = (wq_dn if n % 2 else wq_up)[:, i % 2, :].rearrange("p (b e) -> p b e", e=BLOCK)
                scale = scales[:, i % 4, NB:NB + DB, None] if n % 2 else scales[:, i % 4, 0:NB, None]
                dve.wait_ge(scale_in[i % 4], 16 * (i // 4 + 1))
                dve.wait_ge((qdn_in if n % 2 else qup_in)[i % 2], 16 * (i // 2 + 1))
                nc.vector.scalar_tensor_tensor(out=raw, in0=raw.bitcast(I32), scalar=-ZERO,
                                               in1=scale.broadcast_to([P, D // BLOCK, BLOCK]),
                                               op0=ALU.add, op1=ALU.mult).then_inc(deq_done, 1)

            def split_rows():
                dve.wait_ge(lora_in, 16)
                nc.vector.tensor_copy(rows[:], rows_raw).then_inc(rows_hi, 1)
                dve.wait_ge(rows_hi, 1)
                for a in (0, LORA_DN):
                    nc.vector.tensor_tensor(rows[a:a + 2 * RANK, :], rows_raw[a:a + 2 * RANK, :],
                                            rows[a:a + 2 * RANK, :].bitcast(F32), ALU.subtract).then_inc(rows_lo, 1)
                dve.wait_ge(rows_lo, 2)
                for a in (0, LORA_DN):
                    nc.vector.tensor_copy(rows[a:a + RANK, :], rows_raw[a:a + RANK, :]).then_inc(rows_done, 1)

            def split_cols(i):
                dve.wait_ge(col_in[i % 2], 16 * (i // 2 + 1))
                if i >= 2:
                    dve.wait_ge(wt_done, 2 * (i - 1))
                nc.vector.tensor_copy(cols_split[:, i % 2, :], cols_raw[:, i % 2, :]).then_inc(cols_hi, 1)
                dve.wait_ge(cols_hi, i + 1)
                for a in (2 * RANK, LORA_DN + 2 * RANK):
                    nc.vector.tensor_tensor(cols_split[a:a + RANK, i % 2, :], cols_raw[a:a + RANK, i % 2, :],
                                            cols_split[a:a + RANK, i % 2, :].bitcast(F32),
                                            ALU.subtract).then_inc(cols_done, 1)

            def weight_lo(n):
                i = n // 2
                dve.wait_ge(whi_done, n + 1)
                if n % 2 == 0:
                    cut = slice(i * P, (i + 1) * P)
                    nc.vector.tensor_tensor(up_lo[:, :, cut], weight_bank[n][:].rearrange("p (k h) -> p k h", h=P),
                                            up_hi[:, :, cut].bitcast(F32), ALU.subtract).then_inc(wlo_done, 1)
                else:
                    nc.vector.tensor_tensor(dn_lo[:, i, :], weight_bank[n][:], dn_hi[:, i, :].bitcast(F32),
                                            ALU.subtract).then_inc(wlo_done, 1)

            def prepare(step):
                weight_lo(EARLY + 2 * step)
                if step + 3 < HT:
                    split_cols(step + 3)
                weight_lo(EARLY + 2 * step + 1)

            def stats1(u, js):
                for j in js:
                    dve.wait_ge(x_mix[j], 16 * pair_of(u, js) + 16)
                    nc.vector.bn_stats(st1[:, j, :], mix[:, j, :]).then_inc(bn1_done, 1)
                dve.wait_ge(bn1_done, tokens(u, js) + len(js))
                dve.sem_inc(stats_there, 1)
                for j in js:
                    nc.vector.bn_aggr(mv1[:, j, :], st1[:, j, :]).then_inc(mv1_done, 1)

            def scan(state, step, js, c, done):
                cols = columns(js)
                for a in range(cols.start, cols.stop, SEQ):
                    nc.vector.tensor_tensor_scan(state[:, a + 1:a + SEQ],
                                                 omega[:, c:c + 1].broadcast_to([P, SEQ - 1]),
                                                 step[:, a:a + SEQ - 1], 0.0, ALU.mult,
                                                 ALU.add).then_inc(done, 1 if js == ALL else 2)
                nc.vector.tensor_copy(state[:, cols.start:cols.stop:SEQ],
                                      step[:, cols.start:cols.stop:SEQ]).then_inc(done, 1)

            def denominator(u, js, c):
                done, cols = KT * u + c, columns(js)
                dve.wait_ge(ea_done, done + 1)
                dve.wait_ge(v_in[c % 2], 32 * u + 16 * (c // 2 + 1))
                if js != FIRST or c >= 1:
                    dve.wait_ge(num_done, done)
                nc.vector.tensor_tensor(kv[:, cols], turn[c % 2][:, cols], vin[:, c % 2, cols],
                                        ALU.mult).then_inc(kv_done, 1)
                scan(past, ea, js, c, pastb_done)
                if js != FIRST or c >= 1:
                    dve.wait_ge(wkv_done, done)
                dve.wait_ge(pastb_done, 3 * done + 3)
                nc.vector.scalar_tensor_tensor(out=den[:, cols], in0=turn[c % 2][:, cols], scalar=beta[:, c:c + 1],
                                               in1=past[:, cols], op0=ALU.mult, op1=ALU.add).then_inc(den_done, 1)

            def invert(u, js, c):
                done, cols = KT * u + c, columns(js)
                dve.wait_ge(den_done, done + 1)
                nc.vector.reciprocal(den[:, cols], den[:, cols]).then_inc(rec_done, 1)

            def numerator(u, js, c):
                done, cols = KT * u + c, columns(js)
                dve.wait_ge(kva_done, done + 1)
                scan(past, kva, js, c, pasta_done)
                dve.wait_ge(pasta_done, 3 * done + 3)
                nc.vector.scalar_tensor_tensor(out=mix[:, js[0]:js[-1] + 1, c * P:(c + 1) * P],
                                               in0=kv[:, cols].rearrange("p (j t) -> p j t", t=P),
                                               scalar=beta[:, c:c + 1],
                                               in1=past[:, cols].rearrange("p (j t) -> p j t", t=P),
                                               op0=ALU.mult, op1=ALU.add).then_inc(num_done, 1)

            def norm_stats(u, js, bank):
                done = tokens(u, js) - js[0]
                for a in range(js[0], js[-1] + 1, 2):
                    for j in (a, a + 1):
                        dve.wait_ge(x_in[j], 16 * pair_of(u, js) + 16)
                        dve.wait_ge(yt_done, done + j + 1)
                        nc.vector.tensor_tensor(xin[:, j, :], bank[j % 2][:], xin[:, j, :],
                                                ALU.add).then_inc(x1_done, 1)
                    for j in (a, a + 1):
                        dve.wait_ge(x1_done, done + j + 1)
                        nc.vector.bn_stats(st2[:, j, :], xin[:, j, :]).then_inc(bn2_done, 1)
                dve.wait_ge(bn2_done, done + js[-1] + 1)
                dve.sem_inc(stats_there, 1)
                for j in js:
                    nc.vector.bn_aggr(mv2[:, j, :], st2[:, j, :]).then_inc(mv2_done, 1)

            def norm(u, js):
                dve.wait_ge(ln2_done, u + 1)
                for j in js:
                    nc.vector.tensor_scalar(mix[:, j, :], xin[:, j, :], mv2[:, j, 0:1], rstd2[:, j:j + 1],
                                            ALU.subtract, ALU.mult).then_inc(n_done, 1)

            def norm_lo(u, js, k, bank):
                cols = columns(js)
                dve.wait_ge(nhi_done, KT * u + k + 1)
                nc.vector.tensor_tensor(n_lo[:, k, cols], bank[:, cols], n_hi[:, k, cols].bitcast(F32),
                                        ALU.subtract).then_inc(nlo_done, 1)

            def hidden_lo0(u):
                dve.wait_ge(hhi_done, HT * u + 1)
                nc.vector.tensor_tensor(h_lo[:, 0, :], relu[:], h_hi[:, 0, :].bitcast(F32),
                                        ALU.subtract).then_inc(hlo_done, 1)

            def output(u, js):
                for t in js:
                    dve.wait_ge(res_done, tokens(u, js) + t - js[0] + 1)
                    if t < js[-1]:
                        dve.wait_ge(acc_done, outputs_before(u, js) + t - js[0] + 1)
                    else:
                        dve.wait_ge(down_done, HT * u + HT)
                    nc.vector.tensor_tensor(res[:, t, :], acc[t][:], res[:, t, :], ALU.add).then_inc(out_done, 1)

            stats1(0, FIRST)
            dequantise(0)
            split_rows()
            dve.wait_ge(par_done, 3)
            for c in range(KT):
                denominator(0, FIRST, c)
                invert(0, FIRST, c)
                numerator(0, FIRST, c)
                if c < 2:
                    split_cols(c)
            stats1(1, SECOND)
            norm_stats(0, FIRST, acc)
            weight_lo(0)
            split_cols(2)
            norm(0, FIRST)
            weight_lo(1)
            for k in range(KT):
                norm_lo(0, FIRST, k, n_bank[k])
            weight_lo(2)
            weight_lo(3)

            prepare(0)
            denominator(1, SECOND, 0)
            weight_lo(EARLY + 2)
            invert(1, SECOND, 0)
            split_cols(4)
            weight_lo(EARLY + 3)
            numerator(1, SECOND, 0)
            weight_lo(EARLY + 4)
            denominator(1, SECOND, 1)
            split_cols(5)
            weight_lo(EARLY + 5)
            invert(1, SECOND, 1)
            weight_lo(EARLY + 6)
            numerator(1, SECOND, 1)
            split_cols(6)
            weight_lo(EARLY + 7)
            denominator(1, SECOND, 2)
            weight_lo(EARLY + 8)
            invert(1, SECOND, 2)
            split_cols(7)
            weight_lo(EARLY + 9)
            numerator(1, SECOND, 2)
            weight_lo(EARLY + 10)
            denominator(1, SECOND, 3)
            split_cols(8)
            weight_lo(EARLY + 11)
            invert(1, SECOND, 3)
            weight_lo(EARLY + 12)
            numerator(1, SECOND, 3)
            split_cols(9)
            weight_lo(EARLY + 13)
            norm_stats(1, SECOND, turn)
            prepare(7)
            norm(1, SECOND)
            prepare(8)
            norm_lo(1, SECOND, 0, turn[0])
            norm_lo(1, SECOND, 1, turn[1])
            prepare(9)
            norm_lo(1, SECOND, 2, turn[0])
            norm_lo(1, SECOND, 3, turn[1])
            prepare(10)
            prepare(11)
            stats1(2, ALL)
            prepare(12)
            prepare(13)
            for c in range(KT):
                denominator(2, ALL, c)
                invert(2, ALL, c)
                numerator(2, ALL, c)
                if c == 1:
                    output(0, FIRST)
            norm_stats(2, ALL, turn)
            norm(2, ALL)
            for k in range(KT):
                norm_lo(2, ALL, k, n_bank[k])
            output(1, SECOND)

            def pair(p, is_last):
                u = p + 1
                if not is_last:
                    stats1(u + 1, ALL)
                hidden_lo0(u)
                if not is_last:
                    for c in range(KT):
                        denominator(u + 1, ALL, c)
                        invert(u + 1, ALL, c)
                        numerator(u + 1, ALL, c)
                    norm_stats(u + 1, ALL, turn)
                    norm(u + 1, ALL)
                    for k in range(KT):
                        norm_lo(u + 1, ALL, k, n_bank[k])
                output(u, ALL)

            with dve.Fori(1, NPAIR - 1) as p:
                pair(p, False)
            pair(NPAIR - 1, True)

        @block.tensor
        def _(pe):
            def weights(n):
                i, bank = n // 2, weight_bank[n]
                raw = (wq_dn if n % 2 else wq_up)[:, i % 2, :]
                if n < BY_DVE:
                    pe.wait_ge(deq_done, n + 1)
                else:
                    pe.wait_ge(scaled, n - BY_DVE + 1)
                if n >= EARLY:
                    pe.wait_ge(wlo_done, n - 1)
                for k in range(KT):
                    nc.tensor.matmul(bank[:, k * P:(k + 1) * P], raw[:, k * P:(k + 1) * P], ident[:],
                                     start=(k == 0), stop=False, is_transpose=True, skip_group_check=True)
                pe.wait_ge(cols_done, 2 * i + 2)
                if n % 2 == 0:
                    for k in range(KT):
                        last = nc.tensor.matmul(bank[:, k * P:(k + 1) * P], rows[0:LORA, k * P:(k + 1) * P],
                                                cols_split[0:LORA, i % 2, :], start=False, stop=(k == KT - 1),
                                                skip_group_check=True)
                else:
                    last = nc.tensor.matmul(bank[:], cols_split[LORA_DN:LORA_ROWS, i % 2, :],
                                            rows[LORA_DN:LORA_ROWS, :], start=False, stop=True,
                                            skip_group_check=True)
                last.then_inc(wt_done, 1)

            def turn_e(js, c):
                for j in js:
                    last = nc.tensor.transpose(turn[c % 2][:, j * P:(j + 1) * P], mix[:, j, c * P:(c + 1) * P],
                                               ident[:])
                last.then_inc(et_done, 1)

            def turn_y(j):
                for c in range(KT):
                    last = nc.tensor.transpose(turn[j % 2][:, c * P:(c + 1) * P], mix[:, j, c * P:(c + 1) * P],
                                               ident[:])
                last.then_inc(yt_done, 1)

            def turn_y0(c):
                pe.wait_ge(wkv_done, c + 1)
                for j in FIRST:
                    last = nc.tensor.transpose(acc[j][:, c * P:(c + 1) * P], mix[:, j, c * P:(c + 1) * P], ident[:])
                    if c == KT - 1:
                        last.then_inc(yt_done, 1)

            def turn_n(u, js, k, bank):
                if k == 0:
                    pe.wait_ge(n_done, tokens(u, js) + len(js))
                for j in js:
                    last = nc.tensor.transpose(bank[:, j * P:(j + 1) * P], mix[:, j, k * P:(k + 1) * P], ident[:])
                last.then_inc(nt_done, 1)

            def up(u, js, i):
                cols = columns(js)
                if js != FIRST or i >= 2:
                    pe.wait_ge(relu_done, HT * u + i - 1)
                if js == FIRST:
                    pe.wait_ge(wlo_done, 2 * i + 1)
                cut = slice(i * P, (i + 1) * P)
                for k in range(KT):
                    if i == 0:
                        pe.wait_ge(nlo_done, KT * u + k + 1)
                    nc.tensor.matmul(y1[i % 2][:, cols], up_hi[:, k, cut], n_hi[:, k, cols], start=(k == 0),
                                     stop=False)
                    nc.tensor.matmul(y1[i % 2][:, cols], up_hi[:, k, cut], n_lo[:, k, cols], start=False, stop=False)
                    last = nc.tensor.matmul(y1[i % 2][:, cols], up_lo[:, k, cut], n_hi[:, k, cols], start=False,
                                            stop=(k == KT - 1))
                last.then_inc(up_done, 1)

            def down(u, js, i):
                pe.wait_ge(hlo_done, HT * u + i + 1)
                if js == FIRST:
                    pe.wait_ge(wlo_done, 2 * i + 2)
                for t in js:
                    if i == 0 and js == ALL:
                        pe.wait_ge(out_done, JT * (u - 2) + t + 1)
                    part = slice(t * P, (t + 1) * P)
                    hi, lo = h_hi[:, i % 2, part], h_lo[:, i % 2, part]
                    nc.tensor.matmul(acc[t][:], hi, dn_hi[:, i, :], start=(i == 0), stop=False)
                    nc.tensor.matmul(acc[t][:], hi, dn_lo[:, i, :], start=False, stop=False)
                    last = nc.tensor.matmul(acc[t][:], lo, dn_hi[:, i, :], start=False, stop=(i == HT - 1))
                    if i == HT - 1 and t < js[-1]:
                        last.then_inc(acc_done, 1)
                last.then_inc(down_done, 1)

            pe.wait_ge(id_done, 1)
            pe.wait_ge(e_done, len(FIRST))
            turn_e(FIRST, 0)
            turn_e(FIRST, 1)
            pe.wait_ge(den_done, 1)
            turn_e(FIRST, 2)
            pe.wait_ge(rows_done, 2)
            weights(0)
            turn_y0(0)
            pe.wait_ge(den_done, 2)
            turn_e(FIRST, 3)
            weights(1)
            turn_y0(1)
            weights(2)
            turn_y0(2)
            weights(3)
            turn_y0(3)
            pe.wait_ge(wlo_done, 1)
            pe.wait_ge(den_done, KT)
            for k in range(KT):
                if k == KT - 1:
                    pe.wait_ge(wlo_done, 2)
                turn_n(0, FIRST, k, n_bank[k])

            for i in range(HT):
                n = EARLY + 2 * i
                up(0, FIRST, i)
                if n < 2 * HT:
                    weights(n)
                if i == 0:
                    pe.wait_ge(e_done, JT)
                    pe.wait_ge(nlo_done, 3)
                    turn_e(SECOND, 0)
                    turn_e(SECOND, 1)
                if i in (2, 3):
                    pe.wait_ge(den_done, KT + i - 1)
                    turn_e(SECOND, i)
                if i == 7:
                    pe.wait_ge(wkv_done, 2 * KT)
                    pe.wait_ge(den_done, 2 * KT)
                    turn_y(2)
                    turn_y(3)
                if i == 9:
                    turn_n(1, SECOND, 0, turn[0])
                    turn_n(1, SECOND, 1, turn[1])
                if i == 10:
                    for k in (2, 3):
                        pe.wait_ge(nlo_done, KT + k - 1)
                        turn_n(1, SECOND, k, turn[k % 2])
                if i == HT - 1:
                    pe.wait_ge(e_done, 2 * JT)
                    pe.wait_ge(nlo_done, 2 * KT)
                    turn_e(ALL, 0)
                    turn_e(ALL, 1)
                if i >= 1:
                    down(0, FIRST, i - 1)
                if n < 2 * HT:
                    weights(n + 1)
            down(0, FIRST, HT - 1)
            for i in range(HT):
                if i == HT - 1:
                    pe.wait_ge(relu_done, 2 * HT - 1)
                    for k in range(KT - 1):
                        turn_n(2, ALL, k, n_bank[k])
                up(1, SECOND, i)
                if i in (1, 4):
                    c = (1, 4).index(i) + 2
                    pe.wait_ge(den_done, 2 * KT + c - 1)
                    turn_e(ALL, c)
                if i == 11:
                    pe.wait_ge(wkv_done, 3 * KT)
                    pe.wait_ge(den_done, 3 * KT)
                    turn_y(0)
                    turn_y(1)
                if i == 12:
                    for j in (2, 3):
                        pe.wait_ge(x1_done, JT + j - 1)
                        turn_y(j)
                if i >= 1:
                    down(1, SECOND, i - 1)
            pe.wait_ge(relu_done, 2 * HT)
            turn_n(2, ALL, KT - 1, n_bank[KT - 1])
            down(1, SECOND, HT - 1)

            def pair(p, is_last):
                u = p + 1
                for i in range(HT):
                    if i == HT - 1 and not is_last:
                        pe.wait_ge(relu_done, HT * u + HT - 1)
                        for k in range(KT - 1):
                            turn_n(u + 1, ALL, k, n_bank[k])
                    up(u, ALL, i)
                    if not is_last and 3 <= i < 3 + KT:
                        c = i - 3
                        if c == 0:
                            pe.wait_ge(e_done, JT * u + JT)
                        if c < 2:
                            pe.wait_ge(nlo_done, KT * u + c + 2)
                        else:
                            pe.wait_ge(den_done, KT * (u + 1) + c - 1)
                        turn_e(ALL, c)
                    if not is_last and i in (10, 11):
                        for j in (2 * (i - 10), 2 * (i - 10) + 1):
                            if j == 0:
                                pe.wait_ge(wkv_done, KT * (u + 1) + KT)
                            if j < 2:
                                pe.wait_ge(den_done, KT * (u + 1) + 3 + j)
                            else:
                                pe.wait_ge(x1_done, JT * u + j - 1)
                            turn_y(j)
                    if i >= 1:
                        down(u, ALL, i - 1)
                if not is_last:
                    pe.wait_ge(relu_done, HT * (u + 1))
                    turn_n(u + 1, ALL, KT - 1, n_bank[KT - 1])
                down(u, ALL, HT - 1)

            with pe.Fori(1, NPAIR - 1) as p:
                pair(p, False)
            pair(NPAIR - 1, True)


def kernel(x, ctx_2048, L0_xattn_time_decay, L0_xattn_time_first, L0_ffn_w_up_q, L0_ffn_w_up_scale,
           L0_ffn_b_up, L0_ffn_w_up_lora_a, L0_ffn_w_up_lora_b, L0_ffn_w_down_q, L0_ffn_w_down_scale,
           L0_ffn_b_down, L0_ffn_w_down_lora_a, L0_ffn_w_down_lora_b):
    import numpy as np
    import concourse.bacc as bacc
    from concourse.bass_utils import run_bass_kernel_spmd

    def lay(a):
        return np.ascontiguousarray(a)

    gap = np.zeros((LORA_DN - LORA, 1), np.float32)
    a_up, b_up_l = np.asarray(L0_ffn_w_up_lora_a), np.asarray(L0_ffn_w_up_lora_b)
    a_dn, b_dn_l = np.asarray(L0_ffn_w_down_lora_a), np.asarray(L0_ffn_w_down_lora_b)
    rows = np.concatenate([a_up.T] * 3 + [gap.repeat(D, 1)] + [b_dn_l] * 3)
    cols = np.concatenate([b_up_l] * 3 + [gap.repeat(HID, 1)] + [a_dn.T] * 3)
    arrays = {
        "x": lay(np.asarray(x).reshape(BATCH * SEQ, D)),
        "ctx_t": lay(np.asarray(ctx_2048).transpose(2, 0, 1).reshape(D, BATCH * SEQ)),
        "decay": lay(np.asarray(L0_xattn_time_decay).reshape(KT, P).T),
        "first": lay(np.asarray(L0_xattn_time_first).reshape(KT, P).T),
        "q_up": lay(np.asarray(L0_ffn_w_up_q).reshape(HT, P, D)),
        "q_dn": lay(np.asarray(L0_ffn_w_down_q).reshape(KT, P, HT, P).transpose(2, 1, 0, 3).reshape(HT, P, D)),
        "w_scales": lay(np.concatenate([
            np.asarray(L0_ffn_w_up_scale).reshape(HT, P, NB),
            np.asarray(L0_ffn_w_down_scale).reshape(KT, P, HT, P // BLOCK).transpose(2, 1, 0, 3).reshape(HT, P, DB),
        ], axis=2)),
        "b_up": lay(np.asarray(L0_ffn_b_up).reshape(HT, P).T),
        "b_dn": lay(np.asarray(L0_ffn_b_down).reshape(1, D)),
        "lora_rows": lay(rows),
        "lora_cols": lay(cols.reshape(LORA_ROWS, HT, P).transpose(1, 0, 2)),
    }
    nc = bacc.Bacc("TRN2", target_bir_lowering=False, num_devices=1)
    args = [nc.dram_tensor(f"in_{n}", a.shape, mybir.dt.from_np(a.dtype), kind="ExternalInput").ap()
            for n, a in arrays.items()]
    out = nc.dram_tensor("out", (BATCH * SEQ, D), F32, kind="ExternalOutput").ap()
    build(nc, *args, out)
    done = run_bass_kernel_spmd(nc, [{f"in_{n}": a for n, a in arrays.items()}], core_ids=[0])
    return done.results[0]["out"].reshape(BATCH, SEQ, D)
```
